# Optimizing a Trainium2 kernel written in Bass

```python
import numpy as np
import jax
import jax.numpy as jnp

def _softmax(x, axis=-1):
    return jax.nn.softmax(x, axis=axis)

def _gelu(x):
    return jax.nn.gelu(x, approximate=True)

def _silu(x):
    return jax.nn.silu(x)

def _sigmoid(x):
    return jax.nn.sigmoid(x)

def _layernorm(x, axis=-1, eps=1e-05):
    m = jnp.mean(x, axis=axis, keepdims=True)
    v = jnp.var(x, axis=axis, keepdims=True)
    return (x - m) / jnp.sqrt(v + eps)

def _scatter_add(tgt, idx, src, axis=0):
    return tgt.at[idx].add(src)

def _segment_sum(src, seg, n):
    return jax.ops.segment_sum(src, seg, n)
kernel_name = 'mk_adaln_d1_jaxref_r8_3c0ce7'

def setup_inputs(seed: int=0):
    np.random.seed(seed)
    _w = jnp.asarray

    def _L0_attn_setup():
        import jax, jax.numpy as jnp
        import numpy as np
        BATCH, SEQ = (2, 256)
        HID = 256
        INTER = 512
        STATE = 16
        RANK = 128
        K = 4
        key = jax.random.key(seed)
        ks = jax.random.split(key, 8)
        s = 0.02
        return {'hidden_states': jax.random.normal(ks[0], (BATCH, SEQ, HID), jnp.float32), 'in_proj_w': jax.random.normal(ks[1], (2 * INTER, HID), jnp.float32) * s, 'conv_w': jax.random.normal(ks[2], (INTER, 1, K), jnp.float32) * s, 'conv_b': jnp.zeros((INTER,), jnp.float32), 'x_proj_w': jax.random.normal(ks[3], (RANK + 2 * STATE, INTER), jnp.float32) * s, 'dt_proj_w': jax.random.normal(ks[4], (INTER, RANK), jnp.float32) * s, 'dt_proj_b': jax.random.normal(ks[5], (INTER,), jnp.float32) * s, 'A_log': jnp.log(jnp.broadcast_to(jnp.arange(1, STATE + 1, dtype=jnp.float32), (INTER, STATE))), 'D': jnp.ones((INTER,), jnp.float32), 'out_proj_w': jax.random.normal(ks[6], (HID, INTER), jnp.float32) * s}
    _L0_attn_in = _L0_attn_setup()

    def _L0_ffn_setup():
        import jax, jax.numpy as jnp
        import numpy as np
        H = 256
        E = 64
        I = 64
        SI = 64
        TOP_K = 8
        B, T = (2, 64)
        key = jax.random.key(seed)
        ks = jax.random.split(key, 8)
        s = 0.02
        return {'h': jax.random.normal(ks[0], (B, T, H), jnp.float32), 'gate_w': jax.random.normal(ks[1], (E, H), jnp.float32) * s, 'gu_w': jax.random.normal(ks[2], (E, 2 * I, H), jnp.float32) * s, 'dp_w': jax.random.normal(ks[3], (E, H, I), jnp.float32) * s, 'sh_gate_w': jax.random.normal(ks[4], (SI, H), jnp.float32) * s, 'sh_up_w': jax.random.normal(ks[5], (SI, H), jnp.float32) * s, 'sh_down_w': jax.random.normal(ks[6], (H, SI), jnp.float32) * s, 'sh_gate1_w': jax.random.normal(ks[7], (1, H), jnp.float32) * s}
    _L0_ffn_in = _L0_ffn_setup()
    _L0_c = _w((lambda *s: np.random.randn(*s).astype(np.float32) * 0.05)(1, 256))
    _L0_wmod = _w((lambda *s: np.random.randn(*s).astype(np.float32) * 0.05)(256, 6 * 256) * 256 ** (-0.5))
    _d = {'L0_attn_hidden_states': _L0_attn_in['hidden_states'], 'L0_attn_in_proj_w': _L0_attn_in['in_proj_w'], 'L0_attn_conv_w': _L0_attn_in['conv_w'], 'L0_attn_conv_b': _L0_attn_in['conv_b'], 'L0_attn_x_proj_w': _L0_attn_in['x_proj_w'], 'L0_attn_dt_proj_w': _L0_attn_in['dt_proj_w'], 'L0_attn_dt_proj_b': _L0_attn_in['dt_proj_b'], 'L0_attn_A_log': _L0_attn_in['A_log'], 'L0_attn_D': _L0_attn_in['D'], 'L0_attn_out_proj_w': _L0_attn_in['out_proj_w'], 'L0_ffn_gate_w': _L0_ffn_in['gate_w'], 'L0_ffn_gu_w': _L0_ffn_in['gu_w'], 'L0_ffn_dp_w': _L0_ffn_in['dp_w'], 'L0_ffn_sh_gate_w': _L0_ffn_in['sh_gate_w'], 'L0_ffn_sh_up_w': _L0_ffn_in['sh_up_w'], 'L0_ffn_sh_down_w': _L0_ffn_in['sh_down_w'], 'L0_ffn_sh_gate1_w': _L0_ffn_in['sh_gate1_w'], 'L0_c': _L0_c, 'L0_wmod': _L0_wmod}
    _x0 = _d['L0_attn_hidden_states']
    _d['L0_attn_hidden_states'] = jax.random.normal(jax.random.fold_in(jax.random.key(seed), 1), (1, 2048, 256), dtype=_x0.dtype)
    del _x0
    return _d

def reference(L0_attn_hidden_states, L0_attn_in_proj_w, L0_attn_conv_w, L0_attn_conv_b, L0_attn_x_proj_w, L0_attn_dt_proj_w, L0_attn_dt_proj_b, L0_attn_A_log, L0_attn_D, L0_attn_out_proj_w, L0_ffn_gate_w, L0_ffn_gu_w, L0_ffn_dp_w, L0_ffn_sh_gate_w, L0_ffn_sh_up_w, L0_ffn_sh_down_w, L0_ffn_sh_gate1_w, L0_c, L0_wmod):

    def _L0_attn_ref(hidden_states, in_proj_w, conv_w, conv_b, x_proj_w, dt_proj_w, dt_proj_b, A_log, D, out_proj_w):
        import jax, jax.numpy as jnp
        import numpy as np
        BATCH, SEQ = (2, 256)
        HID = 256
        INTER = 512
        STATE = 16
        RANK = 128
        K = 4
        B, L, _ = hidden_states.shape
        proj = jnp.einsum('blh,ph->blp', hidden_states, in_proj_w)
        u, gate = jnp.split(proj, 2, axis=-1)
        uc = jnp.swapaxes(u, 1, 2)
        conv = jax.lax.conv_general_dilated(uc, conv_w, window_strides=(1,), padding=[(K - 1, 0)], dimension_numbers=('NCH', 'OIH', 'NCH'), feature_group_count=INTER)
        u = jax.nn.silu(conv + conv_b[None, :, None])
        ssm_p = jnp.einsum('bdl,pd->blp', u, x_proj_w).astype(jnp.float32)
        dt_r, Bm, Cm = jnp.split(ssm_p, [RANK, RANK + STATE], axis=-1)
        dt = jax.nn.softplus(jnp.einsum('blr,dr->bld', dt_r, dt_proj_w) + dt_proj_b)
        A = -jnp.exp(A_log)

        def step(state, xs):
            dt_t, B_t, C_t, u_t = xs
            dA = jnp.exp(dt_t[:, :, None] * A[None])
            state = dA * state + (dt_t * u_t)[:, :, None] * B_t[:, None, :]
            y = jnp.einsum('bdn,bn->bd', state, C_t)
            return (state, y)
        xs = (jnp.swapaxes(dt, 0, 1), jnp.swapaxes(Bm, 0, 1), jnp.swapaxes(Cm, 0, 1), jnp.moveaxis(u, 2, 0))
        init = jnp.zeros((B, INTER, STATE), jnp.float32)
        _, ys = jax.lax.scan(step, init, xs)
        y = jnp.moveaxis(ys, 0, 1) + jnp.swapaxes(u, 1, 2) * D[None, None, :]
        y = y * jax.nn.silu(gate)
        return jnp.einsum('bld,hd->blh', y, out_proj_w)

    def _L0_ffn_ref(h, gate_w, gu_w, dp_w, sh_gate_w, sh_up_w, sh_down_w, sh_gate1_w):
        import jax, jax.numpy as jnp
        import numpy as np
        H = 256
        E = 64
        I = 64
        SI = 64
        TOP_K = 8
        B, T = (2, 64)
        Bb, Tt, Hh = h.shape
        x = h.reshape(Bb * Tt, Hh)
        N = x.shape[0]
        logits = x @ gate_w.T
        topv, topi = jax.lax.top_k(logits, TOP_K)
        rw = jax.nn.softmax(topv.astype(jnp.float32), axis=-1).astype(x.dtype)
        W = jnp.zeros((N, E), x.dtype).at[jnp.arange(N)[:, None], topi].set(rw)
        gu = jnp.einsum('nh,eih->nei', x, gu_w)
        gate, up = (gu[..., :I], gu[..., I:])
        inter = jax.nn.silu(gate) * up
        inter_w = inter * W[:, :, None]
        out = jnp.einsum('nei,ehi->nh', inter_w, dp_w)
        sh_inter = jax.nn.silu(x @ sh_gate_w.T) * (x @ sh_up_w.T)
        sh_out = sh_inter @ sh_down_w.T
        sh_g = jax.nn.sigmoid(x @ sh_gate1_w.T)
        out = out + sh_g * sh_out
        return out.reshape(Bb, Tt, Hh)
    x = L0_attn_hidden_states
    mod = (_silu(L0_c) @ L0_wmod).reshape(L0_c.shape[0], 6, 1, -1)
    sa, ca, ga, sb, cb, gb = (mod[:, 0], mod[:, 1], mod[:, 2], mod[:, 3], mod[:, 4], mod[:, 5])
    ga = (2 * (ga >= 0) - 1) * jnp.maximum(jnp.abs(ga), 0.25)
    gb = (2 * (gb >= 0) - 1) * jnp.maximum(jnp.abs(gb), 0.25)
    h = _layernorm(x, axis=-1) * (1 + ca) + sa
    x = x + ga * _L0_attn_ref(h, L0_attn_in_proj_w, L0_attn_conv_w, L0_attn_conv_b, L0_attn_x_proj_w, L0_attn_dt_proj_w, L0_attn_dt_proj_b, L0_attn_A_log, L0_attn_D, L0_attn_out_proj_w)
    h = _layernorm(x, axis=-1) * (1 + cb) + sb
    x = x + gb * _L0_ffn_ref(h, L0_ffn_gate_w, L0_ffn_gu_w, L0_ffn_dp_w, L0_ffn_sh_gate_w, L0_ffn_sh_up_w, L0_ffn_sh_down_w, L0_ffn_sh_gate1_w)
    return x

_drawn_inputs = setup_inputs


def setup_inputs(seed=0):
    import zlib

    import numpy as np

    out = dict(_drawn_inputs(seed))
    spreads = {'L0_attn_conv_b': (0.0, 0.8), 'L0_attn_D': (1.0, 0.6)}
    factors = {'L0_attn_in_proj_w': 8.0,
     'L0_attn_conv_w': 8.0,
     'L0_attn_x_proj_w': 8.0,
     'L0_attn_dt_proj_w': 8.0,
     'L0_attn_dt_proj_b': 8.0,
     'L0_attn_A_log': 8.0,
     'L0_attn_out_proj_w': 8.0,
     'L0_ffn_gate_w': 64.0,
     'L0_ffn_gu_w': 64.0,
     'L0_ffn_dp_w': 64.0,
     'L0_ffn_sh_gate_w': 64.0,
     'L0_ffn_sh_up_w': 64.0,
     'L0_ffn_sh_down_w': 64.0,
     'L0_ffn_sh_gate1_w': 64.0,
     'L0_c': 8.0,
     'L0_wmod': 8.0}
    for name, (base, spread) in spreads.items():
        noise = np.random.default_rng([zlib.crc32(name.encode()), seed]).standard_normal(out[name].shape)
        drawn = base * np.exp(spread * noise) if base else spread * noise
        out[name] = jnp.asarray(drawn.astype(out[name].dtype))
    for name, factor in factors.items():
        out[name] = (out[name] * factor).astype(out[name].dtype)
    return out
```

```python
from contextlib import ExitStack

import concourse.bass as bass
from concourse import mybir

P = 128


def adaln_mamba_moe(nc, x_in, in_proj, conv_w, conv_b, x_proj, dt_proj, dt_b, a_log, d_skip,
                    out_proj, router, pair_w, cond, wmod, out):
    fp32 = mybir.dt.float32
    bf16 = mybir.dt.bfloat16
    u32 = mybir.dt.uint32
    ALU = mybir.AluOpType
    ACT = mybir.ActivationFunctionType
    AX = mybir.AxisListType

    L, H = x_in.shape
    KH = H // P
    DB = conv_b.shape[1]
    TAPS = conv_w.shape[2]
    N = a_log.shape[2]
    R = dt_proj.shape[0]
    E = router.shape[2] - 1
    PAIRS = pair_w.shape[0]
    T = 512
    CH = L // T
    TT = T // P
    EPS = 1e-5
    BODY = 8
    UNITS = DB * N
    SLOTS = 4
    HALVES = 2
    LOADS = [(PAIRS + SLOTS - 1 - s) // SLOTS for s in range(SLOTS)]
    QUSES = [(PAIRS + 1) // 2, PAIRS // 2]
    GU = KH * 2 * P
    assert N == HALVES * BODY and PAIRS == SLOTS * BODY + 1 and DB == 4 and KH == 2 and R == P
    TINY = 2.0 ** -7
    FREE = 1
    CAP = 40.0

    ctx = ExitStack()
    with ctx:
        def sb(name, shape, dt=fp32):
            return ctx.enter_context(nc.sbuf_tensor(name, shape, dt))

        def sem(name):
            return ctx.enter_context(nc.semaphore(name))

        w_in = sb("w_in", [P, KH, 2 * DB * P])
        w_conv = sb("w_conv", [P, DB, TAPS])
        b_conv = sb("b_conv", [P, DB])
        w_xp = sb("w_xp", [P, DB, R + 2 * N])
        w_dt = sb("w_dt", [R, DB * P])
        b_dt = sb("b_dt", [P, DB])
        a_neg = sb("a_neg", [P, DB, N])
        d_sk = sb("d_sk", [P, DB])
        w_out = sb("w_out", [P, DB, H])
        w_rt = sb("w_rt", [P, KH, E + 1])
        ident = sb("ident", [P, P])
        zeros_bf = sb("zeros_bf", [P, T], bf16)
        c_col = sb("c_col", [P, KH])
        c_th = sb("c_th", [P, KH])
        c_rep = sb("c_rep", [P, KH, P])
        ones = sb("ones", [P, P])
        mod_col = sb("mod_col", [P, 6 * KH])
        ga_row = sb("ga_row", [P, 2, H])
        ga_tmp = sb("ga_tmp", [P, 2, H])
        gb_col = sb("gb_col", [P, KH])
        gb_tmp = sb("gb_tmp", [P, KH])
        x_tok = sb("x_tok", [P, TT, H])
        x_norm = sb("x_norm", [P, TT, H])
        x_mid = sb("x_mid", [P, TT, H])
        y_out = sb("y_out", [P, TT, H])
        stats = sb("stats", [P, TT, 6])
        mean_var = sb("mean_var", [P, TT, 2])
        rstd = sb("rstd", [P, TT])
        var_eps = sb("var_eps", [P, TT])
        newton = sb("newton", [P, TT])
        h_attn = sb("h_attn", [P, KH, T])
        h_moe = sb("h_moe", [P, KH, T])
        u_raw = sb("u_raw", [P, DB, TAPS - 1 + T])
        u = sb("u", [P, DB, T])
        z_gate = sb("z_gate", [P, DB, T])
        dt = sb("dt", [P, DB, T])
        dtu = sb("dtu", [P, DB, T])
        y = sb("y", [P, DB, T])
        dt_low = sb("dt_low", [R, T])
        bc_low = sb("bc_low", [2 * N, T])
        tmp_c = sb("tmp_c", [P, DB, T])
        b_rep = sb("b_rep", [P, HALVES, T])
        c_repl = sb("c_repl", [P, HALVES, T])
        d_bu = sb("d_bu", [P, 2, T])
        states = sb("states", [P, HALVES, DB, T])
        prod = sb("prod", [P, 2, T])
        carry = sb("carry", [P, DB, N])
        tmp_a = states[:, 0, :, :]
        tmp_b = states[:, 1, :, :]
        pw = sb("pw", [P, SLOTS, GU + H])
        w_rep = sb("w_rep", [P, SLOTS, T])
        th = sb("th", [P, 2, T])
        act1 = sb("act1", [P, 2, T])
        act2 = sb("act2", [P, 2, T])
        inter = sb("inter", [P, 2, T])
        o_fm = sb("o_fm", [P, KH, T])
        logits = sb("logits", [P, TT, E + 1])
        top8 = sb("top8", [P, TT, 8])
        knocked = sb("knocked", [P, TT, E])
        chosen = sb("chosen", [P, TT, E])
        neg_max = sb("neg_max", [P, TT])
        e_val = sb("e_val", [P, TT, E])
        sh_th = sb("sh_th", [P, TT, 1])
        e_sum = sb("e_sum", [P, TT])
        e_rec = sb("e_rec", [P, TT])
        w_tok = sb("w_tok", [P, TT, E + 2])
        w_fm = sb("w_fm", [E + 2, T])

        bc_dram = nc.dram_tensor("bc_scratch", (2 * N, T), fp32, kind="Internal").ap()
        w_dram = nc.dram_tensor("w_scratch", (E + 2, T), fp32, kind="Internal").ap()

        bank = [ctx.enter_context(nc.psum_tensor(f"bank{i}", [P, T], fp32)) for i in range(8)]
        gate_ps, up_ps, out_ps, da_ps = bank[0:2], bank[2:4], bank[4:6], bank[6:8]
        four = [bank[2], bank[3], bank[6], bank[7]]

        weights_in = sem("weights_in")
        ident_ready = sem("ident_ready")
        dve_setup = sem("dve_setup")
        silu_c_th = sem("silu_c_th")
        silu_c_rep = sem("silu_c_rep")
        mod_ready = sem("mod_ready")
        a_ready = sem("a_ready")
        waits_passed = sem("waits_passed")
        x_arrived = sem("x_arrived")
        x_free = sem("x_free")
        dve_pre = sem("dve_pre")
        dve_post = sem("dve_post")
        var1_ready, var2_ready = sem("var1_ready"), sem("var2_ready")
        ln_ready = sem("ln_ready")
        root1_ready, root2_ready = sem("root1_ready"), sem("root2_ready")
        xn_ready = sem("xn_ready")
        xnT_ready = sem("xnT_ready")
        xn2_ready = sem("xn2_ready")
        xn2T_ready = sem("xn2T_ready")
        ofm_ready = sem("ofm_ready")
        dve_setup_steps = sem("dve_setup_steps")
        h_ready = sem("h_ready")
        inproj_ready = sem("inproj_ready")
        u_evacuated = sem("u_evacuated")
        z_th_ready = sem("z_th_ready")
        hist_saved = sem("hist_saved")
        conv_ready = sem("conv_ready")
        u_th_ready = sem("u_th_ready")
        u_ready = sem("u_ready")
        z_done = sem("z_done")
        xproj_ready = sem("xproj_ready")
        dt_low_ready = sem("dt_low_ready")
        bc_ready = sem("bc_ready")
        bc_written = sem("bc_written")
        dtp_ready = sem("dtp_ready")
        capped = sem("capped")
        e_ready = sem("e_ready")
        log_ready = sem("log_ready")
        scan_in_ready = sem("scan_in_ready")
        b_arrived = [sem(f"b_arrived{i}") for i in range(HALVES)]
        c_arrived = [sem(f"c_arrived{i}") for i in range(HALVES)]
        dbu_done = [sem(f"dbu_done{i}") for i in range(HALVES)]
        da_ready = sem("da_ready")
        scan_done = [sem(f"scan_done{i}") for i in range(2)]
        prod_done = [sem(f"prod_done{i}") for i in range(HALVES)]
        acc_done = sem("acc_done")
        carry_saved = [sem(f"carry_saved{i}") for i in range(HALVES)]
        w_arrived = [sem(f"w_arrived{i}") for i in range(SLOTS)]
        wrep_arrived = [sem(f"wrep_arrived{i}") for i in range(SLOTS)]
        pair_done = [sem(f"pair_done{i}") for i in range(SLOTS)]
        gate_ready = sem("gate_ready")
        up_ready = sem("up_ready")
        th_ready = sem("th_ready")
        act1_ready = sem("act1_ready")
        gu_used = [sem(f"gu_used{i}") for i in range(2)]
        inter_ready = sem("inter_ready")
        moe_ready = sem("moe_ready")
        o_ready = sem("o_ready")
        oT_ready = sem("oT_ready")
        yout_ready = sem("yout_ready")
        stored = sem("stored")
        gated = sem("gated")
        attn_ready = sem("attn_ready")
        logits_ready = sem("logits_ready")
        negmax_ready = sem("negmax_ready")
        e_val_ready = sem("e_val_ready")
        wtok_ready = sem("wtok_ready")
        wT_ready = sem("wT_ready")
        w_fm_ready = sem("w_fm_ready")
        w_written = sem("w_written")
        block = ctx.enter_context(nc.Block())

        def wait_alone(eng, signal, value):
            eng.wait_ge(signal, value)
            eng.sem_inc(waits_passed, 1)

        SA, CA, GA, SB, CB, GB = range(6)

        def col(j, k):
            return mod_col[:, j * KH + k:j * KH + k + 1]

        def wmod_sb(k):
            return (dt, dtu)[k][:].rearrange("p d t -> p (d t)")[:, 0:6 * H]

        @block.sync
        def _(sp):
            small = [(w_in, in_proj), (w_conv, conv_w), (b_conv, conv_b), (w_xp, x_proj),
                     (w_dt, dt_proj), (b_dt, dt_b), (a_neg, a_log), (d_sk, d_skip),
                     (w_out, out_proj), (w_rt, router), (c_col, cond)]
            sp.sem_inc(stored, FREE)
            for k in range(KH):
                sp.dma_start(wmod_sb(k), wmod[:, k, :]).then_inc(weights_in, 16)
            for dst, src in small:
                sp.dma_start(dst[:], src).then_inc(weights_in, 16)

            def load_x(p):
                sp.wait_ge(x_free, p)
                sp.dma_start(x_tok[:], x_in[bass.ts(p, T), :].rearrange("(t p) h -> p t h", p=P)) \
                    .then_inc(x_arrived, 16)

            def write_bc(p):
                for hf in range(HALVES):
                    wait_alone(sp, b_arrived[hf], 16 * BODY * p)
                    wait_alone(sp, c_arrived[hf], 16 * BODY * p)
                sp.wait_ge(bc_ready, p + 1)
                sp.dma_start(bc_dram, bc_low[:]).then_inc(bc_written, 16)
                wait_alone(sp, bc_written, 16 * (p + 1))

            def load_state(p, i, hf):
                g = p * BODY + i
                n = i * HALVES + hf
                wait_alone(sp, dbu_done[hf], g * DB + FREE)
                sp.dma_start(b_rep[:, hf, :], bc_dram[bass.ds(n, 1), :].to_broadcast([P, T])) \
                    .then_inc(b_arrived[hf], 16)
                wait_alone(sp, prod_done[hf], g * DB + FREE)
                sp.dma_start(c_repl[:, hf, :], bc_dram[bass.ds(n + N, 1), :].to_broadcast([P, T])) \
                    .then_inc(c_arrived[hf], 16)

            def load_pair(m, j, s, before):
                wait_alone(sp, pair_done[s], m * LOADS[s] + before + FREE)
                sp.dma_start(pw[:, s, :], pair_w[bass.ds(j, 1), :, :].rearrange("a p n -> (a p) n")) \
                    .then_inc(w_arrived[s], 16)
                for e in range(2):
                    sp.dma_start(w_rep[64 * e:64 * e + 64, s, :],
                                 w_dram[bass.ds(j * 2 + e, 1), :].to_broadcast([64, T])) \
                        .then_inc(wrep_arrived[s], 16)

            def phase(p, scan, moe):
                m = p - 1
                if scan:
                    load_x(p)
                if moe:
                    sp.wait_ge(w_written, 16 * p)
                    load_pair(m, 0, 0, 0)
                if scan:
                    write_bc(p)
                with sp.Fori(0, BODY) as i:
                    for hf in range(HALVES):
                        if scan:
                            load_state(p, i, hf)
                        if moe:
                            for s in (2 * hf, 2 * hf + 1):
                                t = (s + 1) % SLOTS
                                load_pair(m, i * SLOTS + s + 1, t, i + (1 if t == 0 else 0))
                if moe:
                    for k in range(TT // 2):
                        wait_alone(sp, yout_ready, m * (TT // 2) + k + 1)
                    sp.dma_start(out[bass.ts(m, T), :].rearrange("(t p) h -> p t h", p=P), y_out[:]) \
                        .then_inc(stored, 16)
                if scan:
                    for s in range(SLOTS):
                        wait_alone(sp, wrep_arrived[s], 32 * LOADS[s] * p)
                    sp.wait_ge(w_fm_ready, p + 1)
                    sp.dma_start(w_dram, w_fm[:]).then_inc(w_written, 16)

            phase(0, True, False)
            with sp.Fori(1, CH) as p:
                phase(p, True, True)
            phase(CH, False, True)
            sp.wait_ge(stored, 16 * CH + FREE)
            sp.wait_ge(w_written, 16 * CH)
            sp.wait_ge(bc_written, 16 * CH)

        NLOAD = 16 * (KH + 11)

        @block.gpsimd
        def _(pool):
            for signal in prod_done:
                pool.sem_inc(signal, FREE)
            nc.gpsimd.memset(ident[:], 0.0).then_inc(ident_ready, 1)
            pool.wait_ge(ident_ready, 1)
            nc.gpsimd.affine_select(out=ident[:], in_=ident[:], compare_op=ALU.not_equal, fill=1.0, base=0,
                                    pattern=[[-1, P]], channel_multiplier=1).then_inc(ident_ready, 1)

            def body(g):
                for hf in range(HALVES):
                    pool.wait_ge(c_arrived[hf], (g + 1) * 16)
                    for d in range(DB):
                        unit = (g * HALVES + hf) * DB + d
                        pool.wait_ge(scan_done[d % 2], (g * HALVES + hf) * 2 + d // 2 + 1 + FREE)
                        nc.gpsimd.tensor_tensor(prod[:, d % 2, :], states[:, hf, d, :], c_repl[:, hf, :],
                                                ALU.mult).then_inc(prod_done[hf], 1)
                        pool.wait_ge(prod_done[hf], g * DB + d + 1 + FREE)
                        nc.gpsimd.tensor_tensor(y[:, d, :], y[:, d, :], prod[:, d % 2, :],
                                                ALU.add).then_inc(acc_done, 1)
                        pool.wait_ge(acc_done, unit + 1)

            with pool.Fori(0, CH * BODY) as g:
                body(g)

        @block.scalar
        def _(act):
            for signal in carry_saved:
                act.sem_inc(signal, FREE)
            act.wait_ge(weights_in, NLOAD)
            nc.scalar.activation(a_neg[:], a_neg[:], ACT.Exp).then_inc(a_ready, 1)
            nc.scalar.activation(c_th[:], c_col[:], ACT.Tanh, scale=0.5).then_inc(silu_c_th, 1)
            act.wait_ge(dve_setup, 1)

            def modulate(dst, ps, cj, sj, k, done):
                nc.scalar.activation(dst[:, k, :], ps[:], ACT.Identity, bias=col(sj, k), scale=col(cj, k)) \
                    .then_inc(done, 1)

            def root(var_ready, done, p, lns):
                act.wait_ge(var_ready, p + 1)
                nc.scalar.activation(rstd[:], var_eps[:], ACT.Ln).then_inc(ln_ready, 1)
                act.wait_ge(ln_ready, lns + 1)
                nc.scalar.activation(rstd[:], rstd[:], ACT.Exp, scale=-0.5).then_inc(done, 1)

            def pre(p):
                root(var1_ready, root1_ready, p, 2 * p)
                for k in range(KH):
                    act.wait_ge(xnT_ready, p * KH + k + 1)
                    modulate(h_attn, da_ps[k], CA, SA, k, h_ready)
                for b in range(DB):
                    act.wait_ge(inproj_ready, p * 2 * DB + b + 1)
                    if b == 0:
                        act.wait_ge(hist_saved, p + 1)
                    nc.scalar.activation(u_raw[:, b, TAPS - 1:], four[b][:], ACT.Copy).then_inc(u_evacuated, 1)
                for b in range(DB):
                    act.wait_ge(inproj_ready, p * 2 * DB + DB + b + 1)
                    nc.scalar.activation(tmp_a[:, b, :], four[b][:], ACT.Tanh, scale=0.5).then_inc(z_th_ready, 1)
                for b in range(DB):
                    act.wait_ge(conv_ready, p * DB + b + 1)
                    nc.scalar.activation(tmp_c[:, b, :], tmp_b[:, b, :], ACT.Tanh).then_inc(u_th_ready, 1)
                act.wait_ge(xproj_ready, p + 1)
                nc.scalar.activation(dt_low[:], gate_ps[0][:], ACT.Copy).then_inc(dt_low_ready, 1)
                nc.scalar.activation(bc_low[:], gate_ps[1][0:2 * N, :], ACT.Copy).then_inc(bc_ready, 1)
                act.wait_ge(capped, (p + 1) * DB)
                nc.scalar.activation(tmp_a, tmp_b, ACT.Exp).then_inc(e_ready, 1)
                act.wait_ge(e_ready, p + 1)
                nc.scalar.activation(tmp_c[:], tmp_a, ACT.Ln, bias=1.0).then_inc(log_ready, 1)
                act.wait_ge(scan_in_ready, p + 1)

            def decay(p, i, hf, d):
                g = p * BODY + i
                act.wait_ge(scan_done[d % 2], (g * HALVES + hf) * 2 + d // 2 + FREE)
                nc.scalar.activation(da_ps[d % 2][:], dt[:, d, :], ACT.Exp,
                                     scale=a_neg[:, d, bass.ds(i * HALVES + hf, 1)]).then_inc(da_ready, 1)

            def pair_tanh(m, j, q):
                act.wait_ge(gate_ready, m * PAIRS + j + 1)
                nc.scalar.activation(th[:, q, :], gate_ps[q][:], ACT.Tanh, scale=0.5).then_inc(th_ready, 1)

            def save_carry(p, i, hf):
                g = p * BODY + i
                for r in range(2):
                    act.wait_ge(scan_done[r], (g * HALVES + hf + 1) * 2 + FREE)
                nc.scalar.activation(carry[:, :, bass.ds(i * HALVES + hf, 1)], states[:, hf, :, T - 1:T],
                                     ACT.Copy).then_inc(carry_saved[hf], 1)

            def post(p):
                root(var2_ready, root2_ready, p, 2 * p + 1)
                for k in range(KH):
                    act.wait_ge(xn2T_ready, p * KH + k + 1)
                    modulate(h_moe, da_ps[k], CB, SB, k, moe_ready)
                act.wait_ge(negmax_ready, p + 1)
                for t in range(TT):
                    last = nc.scalar.activation(e_val[:, t, :], logits[:, t, 0:E], ACT.Exp, bias=neg_max[:, t:t + 1])
                last = nc.scalar.activation(sh_th[:], logits[:, :, E:E + 1], ACT.Tanh, scale=0.5)
                last.then_inc(e_val_ready, 1)
                act.wait_ge(wT_ready, p + 1)
                nc.scalar.activation(w_fm[:], gate_ps[1][0:E + 2, :], ACT.Copy).then_inc(w_fm_ready, 1)

            def tail(m):
                pair_tanh(m, PAIRS - 1, 0)
                for k in range(KH):
                    act.wait_ge(o_ready, m * KH + k + 1)
                    nc.scalar.activation(o_fm[:, k, :], out_ps[k][:], ACT.Copy,
                                         scale=gb_col[:, k:k + 1]).then_inc(ofm_ready, 1)

            def phase(p, scan, moe):
                if scan:
                    pre(p)
                with act.Fori(0, BODY) as i:
                    for hf in range(HALVES):
                        for r in range(2):
                            if scan:
                                decay(p, i, hf, 2 * r)
                                decay(p, i, hf, 2 * r + 1)
                            if moe:
                                pair_tanh(p - 1, i * SLOTS + 2 * hf + r, r)
                        if scan:
                            save_carry(p, i, hf)
                if moe:
                    tail(p - 1)
                if scan:
                    post(p)

            phase(0, True, False)
            with act.Fori(1, CH) as p:
                phase(p, True, True)
            phase(CH, False, True)

        @block.vector
        def _(dve):
            v = nc.vector

            def steps(counted, base):
                count = [0]

                def step(ins):
                    ins.then_inc(counted, 1)
                    count[0] += 1

                def sync(alone=False):
                    if alone:
                        wait_alone(dve, counted, base + count[0])
                    else:
                        dve.wait_ge(counted, base + count[0])

                return step, sync, count

            def norm(step, sync, src, var_done, root_done, ready, p):
                for t in range(TT):
                    step(v.bn_stats(stats[:, t, :], src[:, t, :]))
                sync(alone=True)
                for t in range(TT):
                    step(v.bn_aggr(mean_var[:, t, :], stats[:, t, :]))
                sync()
                v.tensor_scalar(var_eps[:], mean_var[:, :, 1], EPS, None, ALU.add).then_inc(var_done, 1)
                dve.wait_ge(root_done, p + 1)
                step(v.tensor_tensor(newton[:], rstd[:], rstd[:], ALU.mult))
                sync()
                step(v.tensor_tensor(newton[:], newton[:], var_eps[:], ALU.mult))
                sync()
                step(v.tensor_scalar(newton[:], newton[:], -0.5, 1.5, ALU.mult, ALU.add))
                sync()
                step(v.tensor_tensor(rstd[:], rstd[:], newton[:], ALU.mult))
                sync()
                for t in range(TT):
                    last = v.tensor_scalar(x_norm[:, t, :], src[:, t, :], mean_var[:, t, 0:1], rstd[:, t:t + 1],
                                           ALU.subtract, ALU.mult)
                last.then_inc(ready, 1)

            def setup():
                for signal in dbu_done + scan_done + gu_used:
                    dve.sem_inc(signal, FREE)
                step, sync, count = steps(dve_setup_steps, 0)
                step(v.memset(carry[:], 0.0))
                step(v.memset(u_raw[:], 0.0))
                step(v.memset(zeros_bf[:], 0.0))
                step(v.memset(ones[:], 1.0))
                step(v.memset(w_tok[:], 0.0))
                dve.wait_ge(weights_in, NLOAD)
                dve.wait_ge(silu_c_th, 1)
                step(v.scalar_tensor_tensor(c_col[:], c_th[:], 1.0, c_col[:], ALU.add, ALU.mult))
                sync()
                step(v.tensor_scalar(c_col[:], c_col[:], 0.5, None, ALU.mult))
                sync()
                for k in range(KH):
                    last = v.tensor_scalar(c_rep[:, k, :], ones[:], c_col[:, k:k + 1], None, ALU.mult)
                last.then_inc(silu_c_rep, 1)
                step(v.tensor_scalar(w_conv[:], w_conv[:], 0.5, None, ALU.mult))
                step(v.tensor_scalar(b_conv[:], b_conv[:], 0.5, None, ALU.mult))
                dve.wait_ge(a_ready, 1)
                step(v.tensor_scalar(a_neg[:], a_neg[:], -1.0, None, ALU.mult))
                dve.wait_ge(mod_ready, 1)
                step(v.tensor_copy(mod_col[:], gate_ps[0][:, 0:6 * KH]))
                step(v.tensor_copy(ga_row[:, 0, :], gate_ps[1][:, 0:H]))
                step(v.tensor_copy(ga_row[:, 1, :], gate_ps[1][:, 0:H]))
                sync()
                for j in (CA, CB):
                    step(v.tensor_scalar(mod_col[:, j * KH:j * KH + KH], mod_col[:, j * KH:j * KH + KH],
                                            1.0, None, ALU.add))
                g_col = mod_col[:, GB * KH:GB * KH + KH]
                for g, tmp, dst in ((ga_row[:], ga_tmp, ga_row), (g_col, gb_tmp, gb_col)):
                    step(v.tensor_scalar(tmp[:], g, 0.0, 2.0, ALU.is_ge, ALU.mult))
                    sync()
                    step(v.scalar_tensor_tensor(dst[:], g, -1.0, g, ALU.mult, ALU.max))
                    sync()
                    step(v.tensor_scalar(dst[:], dst[:], 0.25, None, ALU.max))
                    sync()
                    last = v.scalar_tensor_tensor(dst[:], tmp[:], -1.0, dst[:], ALU.add, ALU.mult)
                    if dst is ga_row:
                        step(last)
                last.then_inc(dve_setup, 1)

            NORM = 2 * TT + 4
            PRE = NORM + DB * (TAPS - 1) + 4 + 1 + DB

            def pre(p):
                step, sync, count = steps(dve_pre, p * PRE)
                v.tensor_copy(u_raw[:, :, 0:TAPS - 1], u_raw[:, :, T:T + TAPS - 1]).then_inc(hist_saved, 1)
                dve.wait_ge(x_arrived, (p + 1) * 16)
                norm(step, sync, x_tok, var1_ready, root1_ready, xn_ready, p)
                for b in range(DB):
                    dve.wait_ge(u_evacuated, p * DB + b + 1)
                    step(v.tensor_scalar(tmp_b[:, b, :], u_raw[:, b, TAPS - 1:], w_conv[:, b, TAPS - 1:TAPS],
                                            b_conv[:, b:b + 1], ALU.mult, ALU.add))
                for k in range(TAPS - 1):
                    for b in range(DB):
                        dve.wait_ge(dve_pre, p * PRE + NORM + k * DB + b + 1)
                        ins = v.scalar_tensor_tensor(tmp_b[:, b, :], u_raw[:, b, k:k + T], w_conv[:, b, k:k + 1],
                                                     tmp_b[:, b, :], ALU.mult, ALU.add)
                        if k < TAPS - 2:
                            step(ins)
                        else:
                            ins.then_inc(conv_ready, 1)
                for b in range(DB):
                    dve.wait_ge(u_th_ready, p * DB + b + 1)
                    v.scalar_tensor_tensor(u[:, b, :], tmp_c[:, b, :], 1.0, tmp_b[:, b, :], ALU.add, ALU.mult) \
                        .then_inc(u_ready, 1)
                for b in range(DB):
                    dve.wait_ge(z_th_ready, p * DB + b + 1)
                    v.scalar_tensor_tensor(z_gate[:, b, :], tmp_a[:, b, :], 1.0, four[b][:], ALU.add, ALU.mult) \
                        .then_inc(z_done, 1)
                dve.wait_ge(u_ready, (p + 1) * DB)
                for b in range(DB):
                    v.tensor_scalar(y[:, b, :], u[:, b, :], d_sk[:, b:b + 1], None, ALU.mult)
                for b in range(DB):
                    dve.wait_ge(dtp_ready, p * DB + b + 1)
                    v.tensor_scalar(tmp_b[:, b, :], four[b][:], b_dt[:, b:b + 1], CAP, ALU.add, ALU.min) \
                        .then_inc(capped, 1)
                dve.wait_ge(e_ready, p + 1)
                step(v.tensor_scalar(tmp_b, tmp_a, 1.0 / 3.0, -0.5, ALU.mult, ALU.add))
                step(v.tensor_scalar(dtu[:].bitcast(u32), tmp_a, TINY, None, ALU.is_lt))
                sync()
                step(v.tensor_tensor(tmp_b, tmp_b, tmp_a, ALU.mult))
                sync()
                step(v.scalar_tensor_tensor(tmp_b, tmp_b, 1.0, tmp_a, ALU.add, ALU.mult))
                wait_alone(dve, log_ready, p + 1)
                sync(alone=True)
                step(v.copy_predicated(tmp_c[:], dtu[:].bitcast(u32), tmp_b))
                sync()
                for b in range(DB):
                    step(v.scalar_tensor_tensor(dt[:, b, :], four[b][:], b_dt[:, b:b + 1], tmp_c[:, b, :],
                                                   ALU.add, ALU.max))
                sync()
                assert count[0] == PRE, count
                v.tensor_tensor(dtu[:], dt[:], u[:], ALU.mult).then_inc(scan_in_ready, 1)
                wait_alone(dve, scan_in_ready, p + 1)

            def unit(p, i, hf, d):
                g = p * BODY + i
                n = i * HALVES + hf
                if d == 0:
                    dve.wait_ge(b_arrived[hf], (g + 1) * 16)
                v.tensor_tensor(d_bu[:, d % 2, :], dtu[:, d, :], b_rep[:, hf, :], ALU.mult).then_inc(dbu_done[hf], 1)
                if d == 0:
                    dve.wait_ge(prod_done[hf], g * DB + FREE)
                    dve.wait_ge(carry_saved[hf], g + FREE)
                dve.wait_ge(da_ready, (g * HALVES + hf) * DB + d + 1)
                dve.wait_ge(dbu_done[hf], g * DB + d + 1 + FREE)
                v.tensor_tensor_scan(states[:, hf, d, :], da_ps[d % 2][:], d_bu[:, d % 2, :],
                                     carry[:, d, bass.ds(n, 1)], ALU.mult, ALU.add).then_inc(scan_done[d % 2], 1)

            def pair(m, j, s, quse, arrivals):
                q = s % 2
                count = m * PAIRS + j + 1
                dve.wait_ge(th_ready, count)
                v.scalar_tensor_tensor(act1[:, q, :], th[:, q, :], 1.0, gate_ps[q][:], ALU.add, ALU.mult) \
                    .then_inc(act1_ready, 1)
                dve.wait_ge(up_ready, count)
                dve.wait_ge(act1_ready, count)
                v.tensor_tensor(act2[:, q, :], act1[:, q, :], up_ps[q][:], ALU.mult).then_inc(gu_used[q], 1)
                dve.wait_ge(wrep_arrived[s], (m * LOADS[s] + arrivals) * 32)
                dve.wait_ge(gu_used[q], m * QUSES[q] + quse + FREE)
                o = (s + 2) % SLOTS
                dve.wait_ge(pair_done[o], m * LOADS[o] + arrivals - (1 if s < 2 else 0) + FREE)
                v.tensor_tensor(inter[:, q, :], act2[:, q, :], w_rep[:, s, :], ALU.mult).then_inc(inter_ready, 1)

            def tail(m):
                pair(m, PAIRS - 1, 0, QUSES[0], LOADS[0])
                dve.wait_ge(stored, m * 16 + FREE)
                for k in range(TT // 2):
                    dve.wait_ge(oT_ready, m * (TT // 2) + k + 1)
                    v.tensor_tensor(y_out[:, 2 * k:2 * k + 2, :], x_mid[:, 2 * k:2 * k + 2, :],
                                    gate_ps[k][:].rearrange("p (t h) -> p t h", h=H), ALU.add) \
                        .then_inc(yout_ready, 1)

            POST = TT // 2 + NORM + 1 + 2 * TT + 5

            def post(p):
                step, sync, count = steps(dve_post, p * POST)
                dve.wait_ge(acc_done, (p + 1) * UNITS)
                for b in range(DB):
                    last = v.scalar_tensor_tensor(tmp_a[:, b, :], y[:, b, :], 0.5, z_gate[:, b, :],
                                                  ALU.mult, ALU.mult)
                last.then_inc(gated, 1)
                for k in range(TT // 2):
                    dve.wait_ge(attn_ready, p * (TT // 2) + k + 1)
                    step(v.tensor_tensor(x_mid[:, 2 * k:2 * k + 2, :],
                                            four[k][:].rearrange("p (t h) -> p t h", h=H), ga_row[:], ALU.mult))
                sync()
                for k in range(TT // 2):
                    last = v.tensor_tensor(x_mid[:, 2 * k:2 * k + 2, :], x_mid[:, 2 * k:2 * k + 2, :],
                                           x_tok[:, 2 * k:2 * k + 2, :], ALU.add)
                last.then_inc(x_free, 1)
                dve.wait_ge(x_free, p + 1)
                norm(step, sync, x_mid, var2_ready, root2_ready, xn2_ready, p)
                dve.wait_ge(logits_ready, p + 1)
                step(v.tensor_copy(logits[:].rearrange("p t e -> p (t e)"), gate_ps[0][:, 0:TT * (E + 1)]))
                sync(alone=True)
                for t in range(TT):
                    step(v.max(top8[:, t, :], logits[:, t, 0:E]))
                sync(alone=True)
                for t in range(TT):
                    step(v.match_replace(knocked[:, t, :], top8[:, t, :], logits[:, t, 0:E], -3.0e38))
                v.tensor_scalar(neg_max[:], top8[:, :, 0], -1.0, None, ALU.mult).then_inc(negmax_ready, 1)
                sync()
                step(v.tensor_tensor(chosen[:], knocked[:], logits[:, :, 0:E], ALU.not_equal))
                dve.wait_ge(e_val_ready, p + 1)
                sync()
                step(v.tensor_tensor(e_val[:], e_val[:], chosen[:], ALU.mult))
                step(v.tensor_scalar(w_tok[:, :, E:E + 1], sh_th[:], 1.0, 0.25, ALU.add, ALU.mult))
                sync()
                step(v.tensor_reduce(e_sum[:], e_val[:], AX.X, ALU.add))
                sync()
                step(v.reciprocal(e_rec[:], e_sum[:]))
                sync()
                for t in range(TT):
                    last = v.tensor_scalar(w_tok[:, t, 0:E], e_val[:, t, :], e_rec[:, t:t + 1], 0.5,
                                           ALU.mult, ALU.mult)
                last.then_inc(wtok_ready, 1)
                assert count[0] == POST, count

            def phase(p, scan, moe):
                if scan:
                    pre(p)
                with dve.Fori(0, BODY) as i:
                    for hf in range(HALVES):
                        for r in range(2):
                            if scan:
                                unit(p, i, hf, 2 * r)
                                unit(p, i, hf, 2 * r + 1)
                            if moe:
                                s = 2 * hf + r
                                pair(p - 1, i * SLOTS + s, s, i * 2 + s // 2 + 1, i + 1)
                if moe:
                    tail(p - 1)
                if scan:
                    post(p)

            setup()
            phase(0, True, False)
            with dve.Fori(1, CH) as p:
                phase(p, True, True)
            phase(CH, False, True)

        @block.tensor
        def _(pe):
            mm = nc.tensor.matmul

            def transpose_norm(ready, done, p):
                pe.wait_ge(ready, p + 1)
                for k in range(KH):
                    for t in range(TT):
                        last = nc.tensor.transpose(da_ps[k][:, t * P:(t + 1) * P],
                                                   x_norm[:, t, k * P:(k + 1) * P], ident[:])
                    last.then_inc(done, 1)

            def setup():
                for signal in pair_done:
                    pe.sem_inc(signal, FREE)
                pe.wait_ge(weights_in, NLOAD)
                pe.wait_ge(silu_c_rep, 1)
                for j in range(6 * KH):
                    for k in range(KH):
                        mm(gate_ps[0][:, j:j + 1], wmod_sb(k)[:, j * P:(j + 1) * P], c_rep[:, k, 0:1],
                           start=(k == 0), stop=(k == KH - 1))
                for k in range(KH):
                    last = mm(gate_ps[1][:, 0:H], c_rep[:, k, :], wmod_sb(k)[:, GA * H:(GA + 1) * H],
                              start=(k == 0), stop=(k == KH - 1))
                last.then_inc(mod_ready, 1)
                pe.wait_ge(ident_ready, 2)

            def pre(p):
                transpose_norm(xn_ready, xnT_ready, p)
                pe.wait_ge(h_ready, (p + 1) * KH)
                for b in range(2 * DB):
                    if b >= DB:
                        pe.wait_ge(u_evacuated, p * DB + b - DB + 1)
                    for k in range(KH):
                        last = mm(four[b % DB][:], w_in[:, k, b * P:(b + 1) * P], h_attn[:, k, :],
                                  start=(k == 0), stop=(k == KH - 1))
                    last.then_inc(inproj_ready, 1)
                for b in range(DB):
                    pe.wait_ge(u_ready, p * DB + b + 1)
                    mm(gate_ps[0][:], w_xp[:, b, 0:R], u[:, b, :], start=(b == 0), stop=(b == DB - 1))
                    last = mm(gate_ps[1][0:2 * N, :], w_xp[:, b, R:R + 2 * N], u[:, b, :],
                              start=(b == 0), stop=(b == DB - 1))
                last.then_inc(xproj_ready, 1)
                pe.wait_ge(dt_low_ready, p + 1)
                for b in range(DB):
                    pe.wait_ge(z_done, p * DB + b + 1)
                    mm(four[b][:], w_dt[:, b * P:(b + 1) * P], dt_low[:], start=True, stop=True) \
                        .then_inc(dtp_ready, 1)

            def gate_up(m, s, arrivals, before):
                q = s % 2
                pe.wait_ge(w_arrived[s], (m * LOADS[s] + arrivals) * 16)
                pe.wait_ge(gu_used[q], m * QUSES[q] + before + FREE)
                for ps, o, done in ((gate_ps[q], 0, gate_ready), (up_ps[q], P, up_ready)):
                    for k in range(KH):
                        last = mm(ps[:], pw[:, s, k * 2 * P + o:k * 2 * P + o + P], h_moe[:, k, :],
                                  start=(k == 0), stop=(k == KH - 1))
                    last.then_inc(done, 1)

            def down(m, j, s, stop, done):
                pe.wait_ge(inter_ready, m * PAIRS + j + 1)
                for k in range(KH):
                    last = mm(out_ps[k][:], pw[:, s, GU + k * P:GU + (k + 1) * P], inter[:, s % 2, :],
                              start=False, stop=stop, skip_group_check=True)
                    if done is not None:
                        last.then_inc(done, 1)
                if done is None:
                    last.then_inc(pair_done[s], 1)

            def open_out(m):
                pe.wait_ge(moe_ready, (m + 1) * KH)
                for k in range(KH):
                    mm(out_ps[k][:], zeros_bf[:, 0:P], zeros_bf[:], start=True, stop=False, skip_group_check=True)

            def tail(m):
                down(m, PAIRS - 1, 0, True, o_ready)
                pe.wait_ge(ofm_ready, (m + 1) * KH)
                for t in range(TT):
                    for k in range(KH):
                        last = nc.tensor.transpose(gate_ps[t // 2][:, (t % 2) * H + k * P:(t % 2) * H + (k + 1) * P],
                                                   o_fm[:, k, t * P:(t + 1) * P], ident[:])
                        if t == 0 and k == 0:
                            last.then_inc(pair_done[0], 1)
                    if t % 2:
                        last.then_inc(oT_ready, 1)

            def post(p, moe):
                pe.wait_ge(gated, p + 1)
                for t in range(TT):
                    for b in range(DB):
                        last = mm(four[t // 2][:, (t % 2) * H:(t % 2 + 1) * H], tmp_a[:, b, t * P:(t + 1) * P],
                                  w_out[:, b, :], start=(b == 0), stop=(b == DB - 1))
                    if t % 2:
                        last.then_inc(attn_ready, 1)
                transpose_norm(xn2_ready, xn2T_ready, p)
                pe.wait_ge(moe_ready, (p + 1) * KH)
                if moe:
                    pe.wait_ge(yout_ready, p * (TT // 2))
                W = E + 1
                for t in range(TT):
                    for k in range(KH):
                        last = mm(gate_ps[0][:, t * W:(t + 1) * W], h_moe[:, k, t * P:(t + 1) * P], w_rt[:, k, :],
                                  start=(k == 0), stop=(k == KH - 1))
                last.then_inc(logits_ready, 1)
                pe.wait_ge(wtok_ready, p + 1)
                for t in range(TT):
                    last = nc.tensor.transpose(gate_ps[1][0:E + 2, t * P:(t + 1) * P], w_tok[:, t, :], ident[:])
                last.then_inc(wT_ready, 1)

            def phase(p, scan, moe):
                m = p - 1
                if scan:
                    pre(p)
                if moe:
                    if scan:
                        pe.wait_ge(scan_in_ready, p + 1)
                    else:
                        pe.wait_ge(w_fm_ready, p)
                    open_out(m)
                    gate_up(m, 0, 1, 0)
                    with pe.Fori(0, BODY) as i:
                        for s in range(SLOTS):
                            t = (s + 1) % SLOTS
                            gate_up(m, t, i + (2 if t == 0 else 1), i * 2 + (s + 1) // 2)
                            down(m, i * SLOTS + s, s, False, None)
                    tail(m)
                if scan:
                    post(p, moe)

            setup()
            phase(0, True, False)
            with pe.Fori(1, CH) as p:
                phase(p, True, True)
            phase(CH, False, True)


_OUT = ((1, 2048, 256), "float32")


def kernel(**inputs):
    import numpy as _np
    import concourse.bacc as _bacc
    from concourse import mybir as _mybir
    from concourse.bass_utils import run_bass_kernel_spmd as _run

    def rows(a):
        return _np.ascontiguousarray(a.reshape(a.shape[0] // 128, 128, -1).transpose(1, 0, 2))

    def cols(a):
        return _np.ascontiguousarray(a.reshape(-1, 128).T)

    a = {k: _np.asarray(x) for k, x in inputs.items()}
    gu, dp = a["L0_ffn_gu_w"], a["L0_ffn_dp_w"]
    E, I2, H = gu.shape
    inner = I2 // 2
    gate = _np.concatenate([gu[:, :inner], a["L0_ffn_sh_gate_w"][None], _np.zeros((1, inner, H), gu.dtype)])
    up = _np.concatenate([gu[:, inner:], a["L0_ffn_sh_up_w"][None], _np.zeros((1, inner, H), gu.dtype)])
    down = _np.concatenate([dp, a["L0_ffn_sh_down_w"][None], _np.zeros((1, H, inner), dp.dtype)])
    pairs = (E + 2) // 2

    def lhs(w):
        return w.reshape(pairs, 128, H // 128, 128).transpose(0, 3, 2, 1)

    gate_up = _np.stack([lhs(gate), lhs(up)], axis=3).reshape(pairs, 128, -1)
    downs = down.transpose(0, 2, 1).reshape(pairs, 128, H)
    arrays = {
        "x_in": _np.ascontiguousarray(a["L0_attn_hidden_states"].reshape(-1, H)),
        "in_proj": rows(a["L0_attn_in_proj_w"].T),
        "conv_w": rows(a["L0_attn_conv_w"].reshape(-1, a["L0_attn_conv_w"].shape[2])),
        "conv_b": cols(a["L0_attn_conv_b"]),
        "x_proj": rows(a["L0_attn_x_proj_w"].T),
        "dt_proj": _np.ascontiguousarray(a["L0_attn_dt_proj_w"].T),
        "dt_b": cols(a["L0_attn_dt_proj_b"]),
        "a_log": rows(a["L0_attn_A_log"]),
        "d_skip": cols(a["L0_attn_D"]),
        "out_proj": rows(a["L0_attn_out_proj_w"].T),
        "router": rows(_np.concatenate([a["L0_ffn_gate_w"], a["L0_ffn_sh_gate1_w"]]).T),
        "pair_w": _np.ascontiguousarray(_np.concatenate([gate_up, downs], axis=2)),
        "cond": cols(a["L0_c"].reshape(-1)),
        "wmod": rows(a["L0_wmod"]),
    }
    nc = _bacc.Bacc("TRN2", target_bir_lowering=False, num_devices=1)
    args = [nc.dram_tensor(n, x.shape, _mybir.dt.from_np(x.dtype), kind="ExternalInput").ap()
            for n, x in arrays.items()]
    shape, dtype = _OUT
    out = nc.dram_tensor("out_0_dram", shape, _mybir.dt.from_np(_np.dtype(dtype)), kind="ExternalOutput").ap()
    adaln_mamba_moe(nc, *args, out.rearrange("b l h -> (b l) h"))
    r = _run(nc, [arrays], core_ids=[0])
    return r.results[0]["out_0_dram"]
```

```python
from contextlib import ExitStack

import concourse.bass as bass
from concourse import mybir

P = 128


def adaln_mamba_moe(nc, x_in, in_proj, conv_w, conv_b, x_proj, dt_proj, dt_b, a_log, d_skip,
                    out_proj, router, pair_w, cond, wmod, out):
    fp32 = mybir.dt.float32
    bf16 = mybir.dt.bfloat16
    i32 = mybir.dt.int32
    ALU = mybir.AluOpType
    ACT = mybir.ActivationFunctionType
    AX = mybir.AxisListType

    L, H = x_in.shape
    KH = H // P
    DB = conv_b.shape[1]
    TAPS = conv_w.shape[2]
    N = a_log.shape[2]
    R = dt_proj.shape[0]
    E = router.shape[2] - 1
    PAIRS = pair_w.shape[0]
    T = 512
    CH = L // T
    TT = T // P
    EPS = 1e-5
    BODIES = 8
    SLOTS = 4
    HALVES = 2
    LATE = PAIRS - SLOTS * (BODIES - 1)
    LOADS = [(PAIRS + SLOTS - 1 - s) // SLOTS for s in range(SLOTS)]
    QUSES = [(PAIRS + 1) // 2, PAIRS // 2]
    QUARTERS = SLOTS * BODIES
    GU = KH * 2 * P
    assert N == HALVES * BODIES and PAIRS == QUARTERS + 1 and DB == 4 and KH == 2 and R == P \
        and LATE == 5
    PIECES = KH + DB + 2 + DB
    ROUND = PIECES + DB
    TINY = 2.0 ** -7
    FREE = 1

    ctx = ExitStack()
    with ctx:
        def sb(name, shape, dt=fp32):
            return ctx.enter_context(nc.sbuf_tensor(name, shape, dt))

        def sem(name):
            return ctx.enter_context(nc.semaphore(name))

        w_in = sb("w_in", [P, KH, 2 * DB * P])
        w_conv = sb("w_conv", [P, DB, TAPS])
        b_conv = sb("b_conv", [P, DB])
        w_xp = sb("w_xp", [P, DB, R + 2 * N])
        w_dt = sb("w_dt", [R, DB * P])
        b_dt = sb("b_dt", [P, DB])
        a_neg = sb("a_neg", [P, DB, N])
        d_sk = sb("d_sk", [P, DB])
        w_out = sb("w_out", [P, DB, H])
        w_rt = sb("w_rt", [P, KH, E + 1])
        ident = sb("ident", [P, P])
        zeros_bf = sb("zeros_bf", [P, T], bf16)
        c_col = sb("c_col", [P, KH])
        c_th = sb("c_th", [P, KH])
        c_rep = sb("c_rep", [P, KH, P])
        ones = sb("ones", [P, P])
        root_bias = sb("root_bias", [P, 1])
        mod_col = sb("mod_col", [P, 6 * KH])
        ga_row = sb("ga_row", [P, 2, H])
        gb_col = sb("gb_col", [P, KH])
        gb_tmp = sb("gb_tmp", [P, KH])
        x_tok = [sb(f"x_tok{i}", [P, TT, H]) for i in range(2)]
        x_norm = sb("x_norm", [P, TT, H])
        x_mid = [sb(f"x_mid{i}", [P, TT, H]) for i in range(2)]
        stats = sb("stats", [P, TT, 6])
        mean_var = sb("mean_var", [P, TT, 2])
        rstd = sb("rstd", [P, TT])
        var_eps = sb("var_eps", [P, TT])
        newton = sb("newton", [P, TT])
        h_attn = sb("h_attn", [P, KH, T])
        h_moe = sb("h_moe", [P, KH, T])
        u_raw = sb("u_raw", [P, DB, TAPS - 1 + T])
        u = sb("u", [P, DB, T])
        z_gate = sb("z_gate", [P, DB, T])
        dt = [sb(f"dt{i}", [P, DB, T]) for i in range(2)]
        dtu = sb("dtu", [P, DB, T])
        y = sb("y", [P, DB, T])
        dt_low = sb("dt_low", [R, T])
        bc_low = sb("bc_low", [2 * N, T])
        tmp_a = sb("tmp_a", [P, DB, T])
        tmp_b = sb("tmp_b", [P, DB, T])
        tmp_c = sb("tmp_c", [P, DB, T])
        small_e = x_norm[:, 0:2, :].rearrange("p t h -> p (t h)").bitcast(mybir.dt.uint8) \
            .rearrange("p (d t) -> p d t", t=T)
        ga_tmp = tmp_a[:, 0, :].rearrange("p (t h) -> p t h", h=H)
        b_rep = sb("b_rep", [P, HALVES, T])
        c_repl = sb("c_repl", [P, HALVES, T])
        d_bu = sb("d_bu", [P, 2, T])
        states = sb("states", [P, HALVES, DB, T])
        da = sb("da", [P, 2, T])
        prod = sb("prod", [P, 2, 2, T])
        carry = sb("carry", [P, DB, N])
        pw = sb("pw", [P, SLOTS, GU + H])
        w_rep = sb("w_rep", [P, SLOTS, T])
        act = sb("act", [P, 2, T])
        inter = sb("inter", [P, 2, T])
        o_fm = tmp_b[:, 0:KH, :]
        logits = sb("logits", [P, TT, E + 1])
        top8 = sb("top8", [P, TT, 8])
        knocked = x_norm[:, :, 0:E]
        neg_max = sb("neg_max", [P, TT])
        e_val = x_norm[:, :, E:2 * E]
        sh_th = sb("sh_th", [P, TT, 1])
        e_sum = sb("e_sum", [P, TT])
        w_tok = sb("w_tok", [P, TT, E + 2])
        w_fm = sb("w_fm", [E + 2, T])

        bc_dram = [nc.dram_tensor(f"bc_scratch{i}", (2 * N, T), fp32, kind="Internal").ap() for i in range(2)]
        w_dram = [nc.dram_tensor(f"w_scratch{i}", (E + 2, T), fp32, kind="Internal").ap() for i in range(2)]

        bank = [ctx.enter_context(nc.psum_tensor(f"bank{i}", [P, T], fp32)) for i in range(8)]
        gate_ps, up_ps, out_ps = bank[0:2], bank[2:4], bank[4:6]

        def piece_bank(index):
            return bank[(4 if index < ROUND + PIECES else 6) + index % 2]

        weights_in = sem("weights_in")
        waits_passed = sem("waits_passed")
        ident_ready = sem("ident_ready")
        dve_setup = sem("dve_setup")
        dve_setup_steps = sem("dve_setup_steps")
        silu_c_th = sem("silu_c_th")
        silu_c_rep = sem("silu_c_rep")
        mod_ready = sem("mod_ready")
        a_ready = sem("a_ready")
        x_arrived = sem("x_arrived")
        x_free = sem("x_free")
        dve_pre = sem("dve_pre")
        dve_post = sem("dve_post")
        xn_ready = sem("xn_ready")
        xn2_ready = sem("xn2_ready")
        xn2T_ready = sem("xn2T_ready")
        piece_ready = sem("piece_ready")
        piece_read = sem("piece_read")
        z_ready = sem("z_ready")
        z_done = sem("z_done")
        hist_saved = sem("hist_saved")
        tap_ready = sem("tap_ready")
        conv_ready = sem("conv_ready")
        u_th_ready = sem("u_th_ready")
        u_ready = sem("u_ready")
        y_started = sem("y_started")
        bc_written = sem("bc_written")
        abs_ready = sem("abs_ready")
        series_ready = sem("series_ready")
        e_ready = sem("e_ready")
        log_ready = sem("log_ready")
        dt_ready = sem("dt_ready")
        dtu_ready = sem("dtu_ready")
        b_arrived = [sem(f"b_arrived{i}") for i in range(HALVES)]
        c_arrived = [sem(f"c_arrived{i}") for i in range(HALVES)]
        dbu_done = [sem(f"dbu_done{i}") for i in range(HALVES)]
        da_ready = sem("da_ready")
        scan_done = sem("scan_done")
        prod_done = [sem(f"prod_done{i}") for i in range(HALVES)]
        acc_done = sem("acc_done")
        summed = [sem(f"summed{i}") for i in range(2)]
        carry_saved = [sem(f"carry_saved{i}") for i in range(HALVES)]
        w_arrived = [sem(f"w_arrived{i}") for i in range(SLOTS)]
        wrep_arrived = [sem(f"wrep_arrived{i}") for i in range(SLOTS)]
        pair_done = [sem(f"pair_done{i}") for i in range(SLOTS)]
        gate_ready = sem("gate_ready")
        up_ready = sem("up_ready")
        th_ready = sem("th_ready")
        act1_ready = sem("act1_ready")
        gu_used = [sem(f"gu_used{i}") for i in range(2)]
        inter_ready = sem("inter_ready")
        moe_ready = sem("moe_ready")
        o_ready = sem("o_ready")
        ofm_ready = sem("ofm_ready")
        oT_ready = sem("oT_ready")
        out_ready = sem("out_ready")
        stored = sem("stored")
        gated = sem("gated")
        attn_ready = sem("attn_ready")
        logits_ready = sem("logits_ready")
        negmax_ready = sem("negmax_ready")
        e_val_ready = sem("e_val_ready")
        wtok_ready = sem("wtok_ready")
        wT_ready = sem("wT_ready")
        w_fm_ready = sem("w_fm_ready")
        w_written = sem("w_written")
        block = ctx.enter_context(nc.Block())

        def wait_alone(eng, signal, value):
            eng.wait_ge(signal, value)
            eng.sem_inc(waits_passed, 1)

        SA, CA, GA, SB, CB, GB = range(6)

        def col(j, k):
            return mod_col[:, j * KH + k:j * KH + k + 1]

        def wmod_sb(k):
            return (y, dtu)[k][:].rearrange("p d t -> p (d t)")[:, 0:6 * H]

        NLOAD = 16 * (KH + 11)

        def at_quarters(eng, p, quarter, piece):
            first = BODIES if p < CH - 1 else 3
            for k in range(first * SLOTS):
                quarter(k // SLOTS, k % SLOTS)
                if piece is not None:
                    piece(k)
            if first < BODIES:
                with eng.Fori(first, BODIES) as i:
                    for c in range(SLOTS):
                        quarter(i, c)

        @block.sync
        def _(sp):
            sp.sem_inc(stored, FREE)
            for k in range(KH):
                sp.dma_start(wmod_sb(k), wmod[:, k, :]).then_inc(weights_in, 16)
            for dst, src in [(c_col, cond), (w_in, in_proj), (w_conv, conv_w), (b_conv, conv_b),
                             (w_xp, x_proj), (w_dt, dt_proj), (b_dt, dt_b), (a_neg, a_log), (d_sk, d_skip),
                             (w_out, out_proj), (w_rt, router)]:
                sp.dma_start(dst[:], src).then_inc(weights_in, 16)

            def load_x(c):
                if c >= 2:
                    sp.wait_ge(x_free, c - 1)
                sp.dma_start(x_tok[c % 2][:], x_in[bass.ts(c, T), :].rearrange("(t p) h -> p t h", p=P)) \
                    .then_inc(x_arrived, 16)

            def write_bc(c):
                sp.wait_ge(piece_read, c * ROUND + KH + DB + 2)
                sp.dma_start(bc_dram[c % 2], bc_low[:]).then_inc(bc_written, 16)

            def load_state(p, i, hf):
                g = i + p * BODIES
                n = i * HALVES + hf
                src = bc_dram[p % 2]
                wait_alone(sp, dbu_done[hf], g * 2 + FREE)
                sp.dma_start(b_rep[:, hf, :], src[bass.ds(n, 1), :].to_broadcast([P, T])) \
                    .then_inc(b_arrived[hf], 16)
                wait_alone(sp, prod_done[hf], g * 2 + FREE)
                sp.dma_start(c_repl[:, hf, :], src[bass.ds(n + N, 1), :].to_broadcast([P, T])) \
                    .then_inc(c_arrived[hf], 16)

            def load_weights(m, j, s, before):
                wait_alone(sp, pair_done[s], m * LOADS[s] + before + FREE)
                sp.dma_start(pw[:, s, :], pair_w[bass.ds(j, 1), :, :].rearrange("a p n -> (a p) n")) \
                    .then_inc(w_arrived[s], 16)

            def load_routing(m, j, s):
                for e in range(2):
                    sp.dma_start(w_rep[64 * e:64 * e + 64, s, :],
                                 w_dram[m % 2][bass.ds(j * 2 + e, 1), :].to_broadcast([64, T])) \
                        .then_inc(wrep_arrived[s], 16)

            def store(m):
                sp.wait_ge(out_ready, (m + 1) * (TT // 2))
                sp.dma_start(out[bass.ts(m, T), :].rearrange("(t p) h -> p t h", p=P), x_mid[m % 2][:]) \
                    .then_inc(stored, 16)

            load_x(0)
            write_bc(0)
            for p in range(CH + 1):
                m = p - 1
                scan, moe = p < CH, p > 0
                if p + 1 < CH:
                    load_x(p + 1)
                if scan:
                    sp.wait_ge(bc_written, 16 * (p + 1))

                def quarter(i, c):
                    if scan and c % 2 == 0:
                        load_state(p, i, c // 2)
                    if moe and not (isinstance(i, int) and i <= 1):
                        t = (c + 1) % SLOTS
                        j = (i - 1) * SLOTS + c + 1
                        load_weights(m, j, t, i - 1 + (1 if t == 0 else 0))
                        load_routing(m, j, t)

                def piece(k):
                    if k == 20 and p + 1 < CH:
                        write_bc(p + 1)
                    if moe:
                        if k == 1:
                            for j in range(SLOTS - 1):
                                load_weights(m, j, j, 0)
                        elif k == 2 and m >= 1:
                            store(m - 1)
                        elif k == SLOTS:
                            sp.wait_ge(w_written, 16 * (m + 1))
                            for j in range(SLOTS - 1):
                                load_routing(m, j, j)
                        elif SLOTS + 2 <= k < 2 * SLOTS:
                            j = k - SLOTS + 1
                            load_weights(m, j, j % SLOTS, j // SLOTS)
                            load_routing(m, j, j % SLOTS)

                at_quarters(sp, p, quarter, piece)
                if moe:
                    for j in range(PAIRS - LATE + 1, PAIRS):
                        load_weights(m, j, j % SLOTS, j // SLOTS)
                        load_routing(m, j, j % SLOTS)
            store(CH - 1)
            sp.wait_ge(stored, 16 * CH + FREE)
            sp.wait_ge(w_written, 16 * CH)
            sp.wait_ge(bc_written, 16 * CH)

        @block.gpsimd
        def _(pool):
            for signal in prod_done + carry_saved:
                pool.sem_inc(signal, FREE)
            nc.gpsimd.memset(ident[:], 0.0).then_inc(ident_ready, 1)
            pool.wait_ge(ident_ready, 1)
            nc.gpsimd.affine_select(out=ident[:], in_=ident[:], compare_op=ALU.not_equal, fill=1.0, base=0,
                                    pattern=[[-1, P]], channel_multiplier=1).then_inc(ident_ready, 1)

            def make_dtu(p):
                pool.wait_ge(dt_ready, p + 1)
                if p > 0:
                    for signal in dbu_done:
                        pool.wait_ge(signal, p * QUARTERS // HALVES + FREE)
                nc.gpsimd.tensor_tensor(dtu[:], dt[p % 2][:], u[:], ALU.mult).then_inc(dtu_ready, 1)

            def quarter(p, i, c):
                g, hf, r = i + p * BODIES, c // 2, c % 2
                if r == 0:
                    pool.wait_ge(c_arrived[hf], (g + 1) * 16)
                if p == 0:
                    pool.wait_ge(summed[r], g * 2 + hf + FREE)
                pool.wait_ge(scan_done, g * 2 * SLOTS + 2 * c + 2 + 2 * FREE)
                nc.gpsimd.tensor_tensor(prod[:, r], states[:, hf, 2 * r:2 * r + 2, :],
                                        c_repl[:, hf:hf + 1, :].to_broadcast([P, 2, T]),
                                        ALU.mult).then_inc(prod_done[hf], 1)
                if r == 1:
                    nc.gpsimd.tensor_copy(carry[:, :, bass.ds(i * HALVES + hf, 1)],
                                          states[:, hf, :, T - 1:T]).then_inc(carry_saved[hf], 1)
                if p > 0:
                    pool.wait_ge(prod_done[hf], g * 2 + r + 1 + FREE)
                    nc.gpsimd.tensor_tensor(y[:, 2 * r:2 * r + 2, :], y[:, 2 * r:2 * r + 2, :], prod[:, r],
                                            ALU.add).then_inc(acc_done, 1)

            make_dtu(0)
            with pool.Fori(0, BODIES) as i:
                for c in range(SLOTS):
                    quarter(0, i, c)
            for p in range(1, CH):
                make_dtu(p)
                pool.wait_ge(y_started, p + 1)
                with pool.Fori(0, BODIES) as i:
                    for c in range(SLOTS):
                        quarter(p, i, c)

        @block.scalar
        def _(sca):
            sca.wait_ge(weights_in, NLOAD)
            nc.scalar.activation(a_neg[:], a_neg[:], ACT.Exp).then_inc(a_ready, 1)
            nc.scalar.activation(c_th[:], c_col[:], ACT.Tanh, scale=0.5).then_inc(silu_c_th, 1)
            sca.wait_ge(dve_setup, 1)

            def modulate(dst, ps, cj, sj, k, done):
                nc.scalar.activation(dst[:, k, :], ps[:], ACT.Identity, bias=col(sj, k), scale=col(cj, k)) \
                    .then_inc(done, 1)

            def gate_piece(p, k):
                if 1 <= k < 1 + DB:
                    b = k - 1
                    index = p * ROUND + PIECES + b
                    if b == 0:
                        sca.wait_ge(dt_ready, p + 1)
                        if p > 0:
                            sca.wait_ge(attn_ready, p * (TT // 2))
                    sca.wait_ge(piece_ready, index + 1)
                    nc.scalar.activation(z_gate[:, b, :], piece_bank(index)[:], ACT.Copy).then_inc(z_ready, 1)
                    nc.scalar.activation(tmp_c[:, b, :], piece_bank(index)[:], ACT.Tanh, scale=0.5) \
                        .then_inc(piece_read, 1)

            def pre_piece(c, k):
                first = c * ROUND
                if 6 <= k < 6 + KH:
                    index = first + k - 6
                    sca.wait_ge(piece_ready, index + 1)
                    modulate(h_attn, piece_bank(index), CA, SA, k - 6, piece_read)
                elif 9 <= k < 9 + DB:
                    b = k - 9
                    index = first + KH + b
                    sca.wait_ge(piece_ready, index + 1)
                    sca.wait_ge(hist_saved, c + 1)
                    nc.scalar.activation(tmp_a[:, b, :], piece_bank(index)[:], ACT.Identity,
                                         bias=b_conv[:, b:b + 1], scale=w_conv[:, b, TAPS - 1:TAPS]) \
                        .then_inc(tap_ready, 1)
                    nc.scalar.activation(u_raw[:, b, TAPS - 1:], piece_bank(index)[:], ACT.Copy) \
                        .then_inc(piece_read, 1)
                elif k == 18:
                    index = first + KH + DB
                    sca.wait_ge(piece_ready, index + 1)
                    nc.scalar.activation(dt_low[:], piece_bank(index)[:], ACT.Copy).then_inc(piece_read, 1)
                elif k == 19:
                    index = first + KH + DB + 1
                    if c > 0:
                        sca.wait_ge(bc_written, 16 * c)
                    sca.wait_ge(piece_ready, index + 1)
                    nc.scalar.activation(bc_low[:], piece_bank(index)[0:2 * N, :], ACT.Copy) \
                        .then_inc(piece_read, 1)
                elif 20 <= k < 20 + DB:
                    b = k - 20
                    index = first + KH + DB + 2 + b
                    sca.wait_ge(piece_ready, index + 1)
                    nc.scalar.activation(dt[c % 2][:, b, :], piece_bank(index)[:], ACT.Identity,
                                         bias=b_dt[:, b:b + 1]).then_inc(piece_read, 1)
                elif k == 24:
                    sca.wait_ge(piece_read, first + PIECES)
                    nc.scalar.activation(tmp_a[:], dt[c % 2][:], ACT.Abs).then_inc(abs_ready, 1)
                    sca.wait_ge(abs_ready, c + 1)
                    nc.scalar.activation(tmp_a[:], tmp_a[:], ACT.Exp, scale=-1.0).then_inc(e_ready, 1)
                elif k == 25:
                    sca.wait_ge(e_ready, c + 1)
                    nc.scalar.activation(tmp_b[:], tmp_a[:], ACT.Ln, bias=1.0).then_inc(log_ready, 1)
                    nc.scalar.activation(tmp_c[:], tmp_a[:], ACT.Square, scale=3.0 ** -0.5,
                                         bias=root_bias[:]).then_inc(series_ready, 1)
                if 11 <= k < 11 + DB:
                    b = k - 11
                    sca.wait_ge(conv_ready, c * DB + b + 1)
                    nc.scalar.activation(tmp_b[:, b, :], tmp_a[:, b, :], ACT.Tanh).then_inc(u_th_ready, 1)

            def decay(p, i, c, e):
                unit = (i + p * BODIES) * 2 * SLOTS + 2 * c + e
                d = 2 * (c % 2) + e
                sca.wait_ge(scan_done, unit - 1 + 2 * FREE)
                nc.scalar.activation(da[:, e, :], dt[p % 2][:, d, :], ACT.Exp,
                                     scale=a_neg[:, d, bass.ds(i * HALVES + c // 2, 1)]).then_inc(da_ready, 1)

            def pair_tanh(m, j, q):
                sca.wait_ge(inter_ready, j + m * PAIRS - 1 + 2 * FREE)
                sca.wait_ge(gate_ready, j + m * PAIRS + 1)
                nc.scalar.activation(act[:, q, :], gate_ps[q][:], ACT.Tanh, scale=0.5).then_inc(th_ready, 1)

            def outputs(m):
                for k in range(KH):
                    sca.wait_ge(o_ready, m * KH + k + 1)
                    nc.scalar.activation(o_fm[:, k, :], out_ps[k][:], ACT.Copy,
                                         scale=gb_col[:, k:k + 1]).then_inc(ofm_ready, 1)

            def router(p, k):
                if k == 1:
                    sca.wait_ge(negmax_ready, p + 1)
                    for t in range(TT):
                        nc.scalar.activation(e_val[:, t, :], logits[:, t, 0:E], ACT.Exp,
                                             bias=neg_max[:, t:t + 1])
                    nc.scalar.activation(sh_th[:], logits[:, :, E:E + 1], ACT.Tanh, scale=0.5) \
                        .then_inc(e_val_ready, 1)
                elif k == 3:
                    sca.wait_ge(wT_ready, p + 1)
                    if p > 0:
                        sca.wait_ge(w_written, 16 * p)
                    nc.scalar.activation(w_fm[:], bank[5][0:E + 2, :], ACT.Copy).then_inc(w_fm_ready, 1)
                    sca.wait_ge(w_fm_ready, p + 1)
                    sca.dma_start(w_dram[p % 2], w_fm[:]).then_inc(w_written, 16)

            for k in range(QUARTERS):
                pre_piece(0, k)
            for p in range(CH + 1):
                scan, moe = p < CH, p > 0
                m = p - 1

                def quarter(i, c):
                    if scan:
                        decay(p, i, c, 0)
                    if moe and not (isinstance(i, int) and i == 0):
                        pair_tanh(m, (i - 1) * SLOTS + c, c % 2)
                    if scan:
                        decay(p, i, c, 1)

                def piece(k):
                    if moe:
                        router(m, k)
                    if scan:
                        gate_piece(p, k)
                    if p + 1 < CH:
                        pre_piece(p + 1, k)

                if scan:
                    sca.wait_ge(dt_ready, p + 1)
                    if p > 0:
                        sca.wait_ge(gated, p)
                    for b in range(DB):
                        last = nc.scalar.activation(y[:, b, :], u[:, b, :], ACT.Copy, scale=d_sk[:, b:b + 1])
                    last.then_inc(y_started, 1)
                at_quarters(sca, p, quarter, piece)
                if moe:
                    for j in range(PAIRS - LATE, PAIRS):
                        pair_tanh(m, j, j % 2)
                if scan:
                    for k in range(KH):
                        sca.wait_ge(xn2T_ready, p * KH + k + 1)
                        modulate(h_moe, bank[6 + k], CB, SB, k, moe_ready)
                if moe:
                    outputs(m)

        @block.vector
        def _(dve):
            v = nc.vector

            def steps(counted, base):
                count = [base]

                def step(ins):
                    ins.then_inc(counted, 1)
                    count[0] += 1

                def sync():
                    dve.wait_ge(counted, count[0])

                return step, sync

            pre_step, pre_sync = steps(dve_pre, 0)
            post_step, post_sync = steps(dve_post, 0)

            def norm_stats(step, sync, src):
                for t in range(TT):
                    step(v.bn_stats(stats[:, t, :], src[:, t, :]))
                sync()
                for t in range(TT):
                    step(v.bn_aggr(mean_var[:, t, :], stats[:, t, :]))
                sync()

            def norm_root(step, sync):
                step(v.tensor_scalar(var_eps[:], mean_var[:, :, 1], EPS, None, ALU.add))
                sync()
                step(v.tensor_scalar(newton[:].bitcast(i32), var_eps[:].bitcast(i32), 1, None,
                                     ALU.arith_shift_right))
                sync()
                step(v.tensor_scalar(rstd[:].bitcast(i32), newton[:].bitcast(i32), -1.0, float(0x5F3759DF),
                                     ALU.mult, ALU.add))
                sync()
                for _ in range(3):
                    step(v.tensor_tensor(newton[:], rstd[:], rstd[:], ALU.mult))
                    sync()
                    step(v.scalar_tensor_tensor(newton[:], newton[:], -0.5, var_eps[:], ALU.mult, ALU.mult))
                    sync()
                    step(v.scalar_tensor_tensor(rstd[:], newton[:], 1.5, rstd[:], ALU.add, ALU.mult))
                    sync()

            def norm_apply(src, ready):
                for t in range(TT):
                    last = v.tensor_scalar(x_norm[:, t, :], src[:, t, :], mean_var[:, t, 0:1], rstd[:, t:t + 1],
                                           ALU.subtract, ALU.mult)
                last.then_inc(ready, 1)

            def setup():
                for signal in dbu_done + gu_used:
                    dve.sem_inc(signal, FREE)
                dve.sem_inc(scan_done, 2 * FREE)
                dve.sem_inc(inter_ready, 2 * FREE)
                step, sync = steps(dve_setup_steps, 0)
                step(v.memset(carry[:], 0.0))
                step(v.memset(u_raw[:], 0.0))
                step(v.memset(zeros_bf[:], 0.0))
                step(v.memset(root_bias[:], -(3.0 ** 0.5) / 4.0))
                step(v.memset(ones[:], 1.0))
                step(v.memset(w_tok[:], 0.0))
                dve.wait_ge(weights_in, NLOAD)
                dve.wait_ge(silu_c_th, 1)
                step(v.scalar_tensor_tensor(c_col[:], c_th[:], 1.0, c_col[:], ALU.add, ALU.mult))
                sync()
                step(v.tensor_scalar(c_col[:], c_col[:], 0.5, None, ALU.mult))
                sync()
                for k in range(KH):
                    last = v.tensor_scalar(c_rep[:, k, :], ones[:], c_col[:, k:k + 1], None, ALU.mult)
                last.then_inc(silu_c_rep, 1)
                step(v.tensor_scalar(w_conv[:], w_conv[:], 0.5, None, ALU.mult))
                step(v.tensor_scalar(b_conv[:], b_conv[:], 0.5, None, ALU.mult))
                dve.wait_ge(a_ready, 1)
                step(v.tensor_scalar(a_neg[:], a_neg[:], -1.0, None, ALU.mult))
                dve.wait_ge(mod_ready, 1)
                step(v.tensor_copy(mod_col[:], gate_ps[0][:, 0:6 * KH]))
                step(v.tensor_copy(ga_row[:, 0, :], gate_ps[1][:, 0:H]))
                step(v.tensor_copy(ga_row[:, 1, :], gate_ps[1][:, 0:H]))
                sync()
                for j in (CA, CB):
                    step(v.tensor_scalar(mod_col[:, j * KH:j * KH + KH], mod_col[:, j * KH:j * KH + KH],
                                         1.0, None, ALU.add))
                g_col = mod_col[:, GB * KH:GB * KH + KH]
                for g, tmp, dst in ((ga_row[:], ga_tmp, ga_row[:]), (g_col, gb_tmp[:], gb_col[:])):
                    step(v.tensor_scalar(tmp, g, 0.0, 2.0, ALU.is_ge, ALU.mult))
                    sync()
                    step(v.scalar_tensor_tensor(dst, g, -1.0, g, ALU.mult, ALU.max))
                    sync()
                    step(v.tensor_scalar(dst, dst, 0.25, None, ALU.max))
                    sync()
                    step(v.scalar_tensor_tensor(dst, tmp, -1.0, dst, ALU.add, ALU.mult))
                sync()
                v.tensor_copy(gb_tmp[:], gb_col[:]).then_inc(dve_setup, 1)

            def gate_piece(p, k):
                if 5 <= k < 5 + DB:
                    b = k - 5
                    dve.wait_ge(piece_read, p * ROUND + PIECES + b + 1)
                    v.scalar_tensor_tensor(z_gate[:, b, :], tmp_c[:, b, :], 1.0, z_gate[:, b, :],
                                           ALU.add, ALU.mult).then_inc(z_done, 1)

            def pre_piece(c, k):
                x = x_tok[c % 2]
                dtc = dt[c % 2]
                if k == 1:
                    v.tensor_copy(u_raw[:, :, 0:TAPS - 1], u_raw[:, :, T:T + TAPS - 1]).then_inc(hist_saved, 1)
                elif k == 2:
                    dve.wait_ge(x_arrived, (c + 1) * 16)
                    norm_stats(pre_step, pre_sync, x)
                elif k == 3:
                    norm_root(pre_step, pre_sync)
                elif k == 4:
                    norm_apply(x, xn_ready)
                if 10 <= k < 10 + DB:
                    b = k - 10
                    dve.wait_ge(piece_read, c * ROUND + KH + b + 1)
                    dve.wait_ge(tap_ready, c * DB + b + 1)
                    for tap in range(TAPS - 1):
                        ins = v.scalar_tensor_tensor(tmp_a[:, b, :], u_raw[:, b, tap:tap + T],
                                                     w_conv[:, b, tap:tap + 1], tmp_a[:, b, :],
                                                     ALU.mult, ALU.add)
                        if tap < TAPS - 2:
                            pre_step(ins)
                            pre_sync()
                        else:
                            ins.then_inc(conv_ready, 1)
                if 12 <= k < 12 + DB:
                    b = k - 12
                    dve.wait_ge(u_th_ready, c * DB + b + 1)
                    v.scalar_tensor_tensor(u[:, b, :], tmp_b[:, b, :], 1.0, tmp_a[:, b, :], ALU.add, ALU.mult) \
                        .then_inc(u_ready, 1)
                if 26 <= k < 32:
                    half = slice(0, 2) if k < 29 else slice(2, 4)
                    if k in (26, 29):
                        dve.wait_ge(log_ready, c + 1)
                        dve.wait_ge(series_ready, c + 1)
                        pre_step(v.scalar_tensor_tensor(tmp_c[:, half, :], tmp_c[:, half, :], 13.0 / 16.0,
                                                        tmp_a[:, half, :], ALU.add, ALU.mult))
                        pre_step(v.tensor_scalar(small_e[:, half, :], tmp_a[:, half, :], TINY, None, ALU.is_lt))
                    elif k in (27, 30):
                        pre_sync()
                        pre_step(v.copy_predicated(tmp_b[:, half, :], small_e[:, half, :], tmp_c[:, half, :]))
                    else:
                        pre_sync()
                        last = v.scalar_tensor_tensor(dtc[:, half, :], dtc[:, half, :], 0.0, tmp_b[:, half, :],
                                                      ALU.max, ALU.add)
                        if k == 31:
                            last.then_inc(dt_ready, 1)

            def inputs(p, i, c):
                g, hf, r = i + p * BODIES, c // 2, c % 2
                if r == 0:
                    dve.wait_ge(b_arrived[hf], (g + 1) * 16)
                dve.wait_ge(scan_done, g * 2 * SLOTS + 2 * c + 2 * FREE)
                v.tensor_tensor(d_bu[:], dtu[:, 2 * r:2 * r + 2, :],
                                b_rep[:, hf:hf + 1, :].to_broadcast([P, 2, T]), ALU.mult) \
                    .then_inc(dbu_done[hf], 1)

            def unit(p, i, c, e):
                g, hf, r = i + p * BODIES, c // 2, c % 2
                d = 2 * r + e
                if r == 0 and e == 0:
                    dve.wait_ge(prod_done[hf], g * 2 + FREE)
                    dve.wait_ge(carry_saved[hf], g + FREE)
                if e == 0:
                    dve.wait_ge(dbu_done[hf], g * 2 + r + 1 + FREE)
                dve.wait_ge(da_ready, g * 2 * SLOTS + 2 * c + e + 1)
                v.tensor_tensor_scan(states[:, hf, d, :], da[:, e, :], d_bu[:, e, :],
                                     carry[:, d, bass.ds(i * HALVES + hf, 1)], ALU.mult, ALU.add) \
                    .then_inc(scan_done, 1)

            def pair_gate(m, j, q):
                dve.wait_ge(th_ready, j + m * PAIRS + 1)
                v.scalar_tensor_tensor(act[:, q, :], act[:, q, :], 1.0, gate_ps[q][:], ALU.add, ALU.mult) \
                    .then_inc(act1_ready, 1)

            def pair_up(m, j, q):
                dve.wait_ge(up_ready, j + m * PAIRS + 1)
                dve.wait_ge(act1_ready, j + m * PAIRS + 1)
                v.tensor_tensor(act[:, q, :], act[:, q, :], up_ps[q][:], ALU.mult).then_inc(gu_used[q], 1)

            def pair_weigh(m, s, quse, arrivals):
                q = s % 2
                dve.wait_ge(wrep_arrived[s], (arrivals + m * LOADS[s]) * 32)
                dve.wait_ge(gu_used[q], quse + m * QUSES[q] + FREE)
                o = (s + 2) % SLOTS
                dve.wait_ge(pair_done[o], arrivals + m * LOADS[o] - (1 if s < 2 else 0) + FREE)
                v.tensor_tensor(inter[:, q, :], act[:, q, :], w_rep[:, s, :], ALU.mult).then_inc(inter_ready, 1)

            def finish(m):
                x = x_mid[m % 2]
                for k in range(TT // 2):
                    dve.wait_ge(oT_ready, m * (TT // 2) + k + 1)
                    v.tensor_tensor(x[:, 2 * k:2 * k + 2, :], x[:, 2 * k:2 * k + 2, :],
                                    gate_ps[k][:].rearrange("p (t h) -> p t h", h=H), ALU.add) \
                        .then_inc(out_ready, 1)

            def gating(p):
                if p == 0:
                    dve.wait_ge(y_started, 1)
                    for r in range(2):
                        dve.wait_ge(summed[r], QUARTERS // 2 + FREE)
                    for b in range(DB):
                        post_step(v.tensor_tensor(y[:, b, :], y[:, b, :], bank[b][:], ALU.add))
                    post_sync()
                else:
                    dve.wait_ge(acc_done, p * QUARTERS)
                for b in range(DB):
                    last = v.scalar_tensor_tensor(tmp_c[:, b, :], y[:, b, :], 0.5, z_gate[:, b, :],
                                                  ALU.mult, ALU.mult)
                last.then_inc(gated, 1)

            def residual(p):
                x = x_mid[p % 2]
                if p >= 2:
                    dve.wait_ge(stored, (p - 1) * 16 + FREE)
                for k in range(TT // 2):
                    dve.wait_ge(attn_ready, p * (TT // 2) + k + 1)
                    post_step(v.tensor_tensor(x[:, 2 * k:2 * k + 2, :],
                                              bank[6 + k][:].rearrange("p (t h) -> p t h", h=H), ga_row[:],
                                              ALU.mult))
                post_sync()
                for k in range(TT // 2):
                    last = v.tensor_tensor(x[:, 2 * k:2 * k + 2, :], x[:, 2 * k:2 * k + 2, :],
                                           x_tok[p % 2][:, 2 * k:2 * k + 2, :], ALU.add)
                last.then_inc(x_free, 1)
                dve.wait_ge(x_free, p + 1)
                norm_stats(post_step, post_sync, x)
                norm_root(post_step, post_sync)
                norm_apply(x, xn2_ready)

            def router(p, k):
                if k == 0:
                    dve.wait_ge(logits_ready, p + 1)
                    post_step(v.tensor_copy(logits[:].rearrange("p t e -> p (t e)"),
                                            bank[4][:, 0:TT * (E + 1)]))
                    post_sync()
                    for t in range(TT):
                        post_step(v.max(top8[:, t, :], logits[:, t, 0:E]))
                    post_sync()
                    v.tensor_scalar(neg_max[:], top8[:, :, 0], -1.0, None, ALU.mult).then_inc(negmax_ready, 1)
                elif k == 1:
                    for t in range(TT):
                        post_step(v.match_replace(knocked[:, t, :], top8[:, t, :], logits[:, t, 0:E], -3.0e38))
                    post_sync()
                    post_step(v.tensor_tensor(knocked, knocked, logits[:, :, 0:E], ALU.not_equal))
                elif k == 2:
                    dve.wait_ge(e_val_ready, p + 1)
                    post_sync()
                    post_step(v.tensor_tensor(e_val, e_val, knocked, ALU.mult))
                    post_step(v.tensor_scalar(w_tok[:, :, E:E + 1], sh_th[:], 1.0, 0.25, ALU.add, ALU.mult))
                    post_sync()
                    post_step(v.tensor_reduce(e_sum[:], e_val, AX.X, ALU.add))
                    post_sync()
                    post_step(v.reciprocal(e_sum[:], e_sum[:]))
                    post_sync()
                    for t in range(TT):
                        last = v.tensor_scalar(w_tok[:, t, 0:E], e_val[:, t, :], e_sum[:, t:t + 1], 0.5,
                                               ALU.mult, ALU.mult)
                    last.then_inc(wtok_ready, 1)

            def late_pair(m, j):
                pair_gate(m, j, j % 2)
                pair_up(m, j, j % 2)
                pair_weigh(m, j % SLOTS, j // 2 + 1, j // SLOTS + 1)

            setup()
            for k in range(QUARTERS):
                pre_piece(0, k)
            for p in range(CH + 1):
                scan, moe = p < CH, p > 0
                m = p - 1
                if scan:
                    dve.wait_ge(dtu_ready, p + 1)

                def quarter(i, c):
                    pair = moe and not (isinstance(i, int) and i == 0)
                    j = (i - 1) * SLOTS + c
                    if scan:
                        inputs(p, i, c)
                    if pair:
                        pair_gate(m, j, c % 2)
                    if scan:
                        unit(p, i, c, 0)
                    if pair:
                        pair_up(m, j, c % 2)
                    if scan:
                        unit(p, i, c, 1)
                    if pair:
                        pair_weigh(m, c, (i - 1) * 2 + c // 2 + 1, i)

                def piece(k):
                    if moe:
                        router(m, k)
                        if m >= 1 and k == 1:
                            finish(m - 1)
                    if scan:
                        gate_piece(p, k)
                    if p + 1 < CH:
                        pre_piece(p + 1, k)

                at_quarters(dve, p, quarter, piece)
                late = list(range(PAIRS - LATE, PAIRS)) if moe else []
                for j in late[:2]:
                    late_pair(m, j)
                if scan:
                    gating(p)
                for j in late[2:3]:
                    late_pair(m, j)
                if scan:
                    residual(p)
                for j in late[3:]:
                    late_pair(m, j)
            finish(CH - 1)

        @block.tensor
        def _(pe):
            mm = nc.tensor.matmul

            def setup():
                for signal in pair_done + summed:
                    pe.sem_inc(signal, FREE)
                pe.wait_ge(weights_in, NLOAD)
                pe.wait_ge(silu_c_rep, 1)
                for j in range(6 * KH):
                    for k in range(KH):
                        mm(gate_ps[0][:, j:j + 1], wmod_sb(k)[:, j * P:(j + 1) * P], c_rep[:, k, 0:1],
                           start=(k == 0), stop=(k == KH - 1))
                for k in range(KH):
                    last = mm(gate_ps[1][:, 0:H], c_rep[:, k, :], wmod_sb(k)[:, GA * H:(GA + 1) * H],
                              start=(k == 0), stop=(k == KH - 1))
                last.then_inc(mod_ready, 1)
                pe.wait_ge(ident_ready, 2)

            def piece_free(index):
                if index > 1:
                    pe.wait_ge(piece_read, index - 1)

            def in_proj_piece(index, b):
                piece_free(index)
                for kh in range(KH):
                    last = mm(piece_bank(index)[:], w_in[:, kh, b * P:(b + 1) * P], h_attn[:, kh, :],
                              start=(kh == 0), stop=(kh == KH - 1))
                last.then_inc(piece_ready, 1)

            def gate_piece(p, k):
                if k < DB:
                    in_proj_piece(p * ROUND + PIECES + k, DB + k)

            def pre_piece(c, k):
                first = c * ROUND
                if 5 <= k < 5 + KH:
                    kh = k - 5
                    index = first + kh
                    piece_free(index)
                    pe.wait_ge(xn_ready, c + 1)
                    for t in range(TT):
                        last = nc.tensor.transpose(piece_bank(index)[:, t * P:(t + 1) * P],
                                                   x_norm[:, t, kh * P:(kh + 1) * P], ident[:])
                    last.then_inc(piece_ready, 1)
                elif 8 <= k < 8 + DB:
                    if k == 8:
                        pe.wait_ge(piece_read, first + KH)
                    in_proj_piece(first + KH + k - 8, k - 8)
                elif k in (17, 18):
                    index = first + KH + DB + k - 17
                    piece_free(index)
                    pe.wait_ge(u_ready, (c + 1) * DB)
                    rows = slice(0, R) if k == 17 else slice(R, R + 2 * N)
                    dst = piece_bank(index)[:] if k == 17 else piece_bank(index)[0:2 * N, :]
                    for b in range(DB):
                        last = mm(dst, w_xp[:, b, rows], u[:, b, :], start=(b == 0), stop=(b == DB - 1))
                    last.then_inc(piece_ready, 1)
                elif 19 <= k < 19 + DB:
                    b = k - 19
                    index = first + KH + DB + 2 + b
                    piece_free(index)
                    pe.wait_ge(piece_read, first + KH + DB + 1)
                    mm(piece_bank(index)[:], w_dt[:, b * P:(b + 1) * P], dt_low[:], start=True, stop=True) \
                        .then_inc(piece_ready, 1)

            def gate_up(m, s, arrivals, before):
                q = s % 2
                pe.wait_ge(w_arrived[s], (arrivals + m * LOADS[s]) * 16)
                pe.wait_ge(gu_used[q], before + m * QUSES[q] + FREE)
                for ps, o, done in ((gate_ps[q], 0, gate_ready), (up_ps[q], P, up_ready)):
                    for k in range(KH):
                        last = mm(ps[:], pw[:, s, k * 2 * P + o:k * 2 * P + o + P], h_moe[:, k, :],
                                  start=(k == 0), stop=(k == KH - 1))
                    last.then_inc(done, 1)

            def down(m, j, s, stop):
                pe.wait_ge(inter_ready, j + m * PAIRS + 1 + 2 * FREE)
                for k in range(KH):
                    last = mm(out_ps[k][:], pw[:, s, GU + k * P:GU + (k + 1) * P], inter[:, s % 2, :],
                              start=False, stop=stop, skip_group_check=True)
                    if stop:
                        last.then_inc(o_ready, 1)
                if not stop:
                    last.then_inc(pair_done[s], 1)

            def open_sums(banks):
                for ps in banks:
                    mm(ps[:], zeros_bf[:, 0:P], zeros_bf[:], start=True, stop=False, skip_group_check=True)

            def sum_states(i, c):
                hf, r = c // 2, c % 2
                pe.wait_ge(prod_done[hf], i * 2 + r + 1 + FREE)
                for e in range(2):
                    last = mm(bank[2 * r + e][:], ident[:], prod[:, r, e, :], start=False, stop=False,
                              skip_group_check=True)
                last.then_inc(summed[r], 1)

            def out_transposes(m):
                pe.wait_ge(ofm_ready, (m + 1) * KH)
                for t in range(TT):
                    for k in range(KH):
                        last = nc.tensor.transpose(gate_ps[t // 2][:, (t % 2) * H + k * P:(t % 2) * H + (k + 1) * P],
                                                   o_fm[:, k, t * P:(t + 1) * P], ident[:])
                        if t == 0 and k == 0:
                            last.then_inc(pair_done[0], 1)
                    if t % 2:
                        last.then_inc(oT_ready, 1)

            def attn_out(p):
                pe.wait_ge(gated, p + 1)
                for t in range(TT):
                    for b in range(DB):
                        last = mm(bank[6 + t // 2][:, (t % 2) * H:(t % 2 + 1) * H],
                                  tmp_c[:, b, t * P:(t + 1) * P],
                                  w_out[:, b, :], start=(b == 0), stop=(b == DB - 1))
                    if t % 2:
                        last.then_inc(attn_ready, 1)

            def norm_transposes(p):
                pe.wait_ge(xn2_ready, p + 1)
                for k in range(KH):
                    for t in range(TT):
                        last = nc.tensor.transpose(bank[6 + k][:, t * P:(t + 1) * P],
                                                   x_norm[:, t, k * P:(k + 1) * P], ident[:])
                    last.then_inc(xn2T_ready, 1)

            def router(p, k):
                if k == 0:
                    pe.wait_ge(moe_ready, (p + 1) * KH)
                    for t in range(TT):
                        for kh in range(KH):
                            last = mm(bank[4][:, t * (E + 1):(t + 1) * (E + 1)],
                                      h_moe[:, kh, t * P:(t + 1) * P], w_rt[:, kh, :],
                                      start=(kh == 0), stop=(kh == KH - 1))
                    last.then_inc(logits_ready, 1)
                elif k == 3:
                    pe.wait_ge(wtok_ready, p + 1)
                    for t in range(TT):
                        last = nc.tensor.transpose(bank[5][0:E + 2, t * P:(t + 1) * P], w_tok[:, t, :], ident[:])
                    last.then_inc(wT_ready, 1)

            def late(m, j):
                gate_up(m, j % SLOTS, j // SLOTS + 1, j // 2)

            setup()
            for k in range(QUARTERS):
                pre_piece(0, k)
            for p in range(CH + 1):
                scan, moe = p < CH, p > 0
                m = p - 1
                if not moe:
                    open_sums(bank[0:DB])

                def quarter(i, c):
                    if not moe:
                        sum_states(i, c)
                    elif not isinstance(i, int) or i > 0:
                        t = (c + 1) % SLOTS
                        gate_up(m, t, i + (1 if t == 0 else 0), (i - 1) * 2 + (c + 1) // 2)
                        if not isinstance(i, int) or i > 1 or c > 0:
                            down(m, (i - 1) * SLOTS + c - 1, (c - 1) % SLOTS, False)

                def piece(k):
                    if moe:
                        if m >= 1 and k == 0:
                            out_transposes(m - 1)
                        router(m, k)
                        if k == 3:
                            if m >= 1:
                                pe.wait_ge(out_ready, m * (TT // 2))
                            gate_up(m, 0, 1, 0)
                        elif k == SLOTS:
                            pe.wait_ge(w_fm_ready, p)
                            open_sums(out_ps)
                    if scan:
                        gate_piece(p, k)
                    if p + 1 < CH:
                        pre_piece(p + 1, k)

                at_quarters(pe, p, quarter, piece)
                last = PAIRS - 1
                if moe:
                    late(m, last - 3)
                    down(m, last - 5, (last - 5) % SLOTS, False)
                    late(m, last - 2)
                    down(m, last - 4, (last - 4) % SLOTS, False)
                if scan:
                    attn_out(p)
                if moe:
                    down(m, last - 3, (last - 3) % SLOTS, False)
                    late(m, last - 1)
                    down(m, last - 2, (last - 2) % SLOTS, False)
                    late(m, last)
                if scan:
                    norm_transposes(p)
                if moe:
                    down(m, last - 1, (last - 1) % SLOTS, False)
                    down(m, last, last % SLOTS, True)
            out_transposes(CH - 1)


_OUT = ((1, 2048, 256), "float32")


def kernel(**inputs):
    import numpy as _np
    import concourse.bacc as _bacc
    from concourse import mybir as _mybir
    from concourse.bass_utils import run_bass_kernel_spmd as _run

    def rows(a):
        return _np.ascontiguousarray(a.reshape(a.shape[0] // 128, 128, -1).transpose(1, 0, 2))

    def cols(a):
        return _np.ascontiguousarray(a.reshape(-1, 128).T)

    a = {k: _np.asarray(x) for k, x in inputs.items()}
    gu, dp = a["L0_ffn_gu_w"], a["L0_ffn_dp_w"]
    E, I2, H = gu.shape
    inner = I2 // 2
    gate = _np.concatenate([gu[:, :inner], a["L0_ffn_sh_gate_w"][None], _np.zeros((1, inner, H), gu.dtype)])
    up = _np.concatenate([gu[:, inner:], a["L0_ffn_sh_up_w"][None], _np.zeros((1, inner, H), gu.dtype)])
    down = _np.concatenate([dp, a["L0_ffn_sh_down_w"][None], _np.zeros((1, H, inner), dp.dtype)])
    pairs = (E + 2) // 2

    def lhs(w):
        return w.reshape(pairs, 128, H // 128, 128).transpose(0, 3, 2, 1)

    gate_up = _np.stack([lhs(gate), lhs(up)], axis=3).reshape(pairs, 128, -1)
    downs = down.transpose(0, 2, 1).reshape(pairs, 128, H)
    arrays = {
        "x_in": _np.ascontiguousarray(a["L0_attn_hidden_states"].reshape(-1, H)),
        "in_proj": rows(a["L0_attn_in_proj_w"].T),
        "conv_w": rows(a["L0_attn_conv_w"].reshape(-1, a["L0_attn_conv_w"].shape[2])),
        "conv_b": cols(a["L0_attn_conv_b"]),
        "x_proj": rows(a["L0_attn_x_proj_w"].T),
        "dt_proj": _np.ascontiguousarray(a["L0_attn_dt_proj_w"].T),
        "dt_b": cols(a["L0_attn_dt_proj_b"]),
        "a_log": rows(a["L0_attn_A_log"]),
        "d_skip": cols(a["L0_attn_D"]),
        "out_proj": rows(a["L0_attn_out_proj_w"].T),
        "router": rows(_np.concatenate([a["L0_ffn_gate_w"], a["L0_ffn_sh_gate1_w"]]).T),
        "pair_w": _np.ascontiguousarray(_np.concatenate([gate_up, downs], axis=2)),
        "cond": cols(a["L0_c"].reshape(-1)),
        "wmod": rows(a["L0_wmod"]),
    }
    nc = _bacc.Bacc("TRN2", target_bir_lowering=False, num_devices=1)
    args = [nc.dram_tensor(n, x.shape, _mybir.dt.from_np(x.dtype), kind="ExternalInput").ap()
            for n, x in arrays.items()]
    shape, dtype = _OUT
    out = nc.dram_tensor("out_0_dram", shape, _mybir.dt.from_np(_np.dtype(dtype)), kind="ExternalOutput").ap()
    adaln_mamba_moe(nc, *args, out.rearrange("b l h -> (b l) h"))
    r = _run(nc, [arrays], core_ids=[0])
    return r.results[0]["out_0_dram"]
```

```python
from contextlib import ExitStack

import concourse.bass as bass
from concourse import mybir

P = 128


def adaln_mamba_moe(nc, x_in, in_proj, conv_w, conv_b, x_proj, dt_proj, dt_b, a_log, d_skip,
                    out_proj, router, pair_w, cond, wmod, out):
    fp32 = mybir.dt.float32
    bf16 = mybir.dt.bfloat16
    i32 = mybir.dt.int32
    ALU = mybir.AluOpType
    ACT = mybir.ActivationFunctionType
    AX = mybir.AxisListType

    L, H = x_in.shape
    KH = H // P
    DB = conv_b.shape[1]
    TAPS = conv_w.shape[2]
    N = a_log.shape[2]
    R = dt_proj.shape[0]
    E = router.shape[2] - 1
    PAIRS = pair_w.shape[0]
    T = 512
    CH = L // T
    TT = T // P
    EPS = 1e-5
    BODIES = 8
    SLOTS = 4
    HALVES = 2
    LAST_BODIES = 3
    SH = 64
    LOGS = 25
    SHARED = 4
    LATE = PAIRS - SLOTS * (BODIES - 1)
    LOADS = [(PAIRS + SLOTS - 1 - s) // SLOTS for s in range(SLOTS)]
    QUARTERS = SLOTS * BODIES
    GU = KH * 2 * P
    assert N == HALVES * BODIES and PAIRS == QUARTERS + 1 and DB == 4 and KH == 2 and R == P \
        and LATE == 5
    PIECES = KH + DB + 2 + DB
    ROUND = PIECES + DB
    TINY = 2.0 ** -7
    FREE = 1

    ctx = ExitStack()
    with ctx:
        def sb(name, shape, dt=fp32):
            return ctx.enter_context(nc.sbuf_tensor(name, shape, dt))

        def sem(name):
            return ctx.enter_context(nc.semaphore(name))

        w_in = sb("w_in", [P, KH, 2 * DB * P])
        w_conv = sb("w_conv", [P, DB, TAPS])
        b_conv = sb("b_conv", [P, DB])
        w_xp = sb("w_xp", [P, DB, R + 2 * N])
        w_dt = sb("w_dt", [R, DB * P])
        b_dt = sb("b_dt", [P, DB])
        a_neg = sb("a_neg", [P, DB, N])
        d_sk = sb("d_sk", [P, DB])
        w_out = sb("w_out", [P, DB, H])
        w_rt = sb("w_rt", [P, KH, E + 1])
        ident = sb("ident", [P, P])
        zeros_bf = sb("zeros_bf", [P, T], bf16)
        c_col = sb("c_col", [P, KH])
        c_th = sb("c_th", [P, KH])
        c_rep = sb("c_rep", [P, KH, P])
        ones = sb("ones", [P, P])
        root_bias = sb("root_bias", [P, 1])
        mod_col = sb("mod_col", [P, 6 * KH])
        ga_row = sb("ga_row", [P, 2, H])
        gb_col = sb("gb_col", [P, KH])
        gb_tmp = sb("gb_tmp", [P, KH])
        x_tok = [sb(f"x_tok{i}", [P, TT, H]) for i in range(2)]
        x_norm = sb("x_norm", [P, TT, H])
        x_mid = [sb(f"x_mid{i}", [P, TT, H]) for i in range(2)]
        stats = sb("stats", [P, TT, 6])
        mean_var = sb("mean_var", [P, TT, 2])
        rstd = sb("rstd", [P, TT])
        var_eps = sb("var_eps", [P, TT])
        newton = sb("newton", [P, TT])
        h_attn = sb("h_attn", [P, KH, T])
        h_moe = sb("h_moe", [P, KH, T])
        u_raw = sb("u_raw", [P, DB, TAPS - 1 + T])
        u = sb("u", [P, DB, T])
        z_gate = sb("z_gate", [P, DB, T])
        dt = [sb(f"dt{i}", [P, DB, T]) for i in range(2)]
        dtu = sb("dtu", [P, DB, T])
        y = sb("y", [P, DB, T])
        dt_low = sb("dt_low", [R, T])
        bc_low = sb("bc_low", [2 * N, T])
        tmp_a = sb("tmp_a", [P, DB, T])
        tmp_b = sb("tmp_b", [P, DB, T])
        tmp_c = sb("tmp_c", [P, DB, T])
        small_e = x_norm[:, 0:2, :].rearrange("p t h -> p (t h)").bitcast(mybir.dt.uint8) \
            .rearrange("p (d t) -> p d t", t=T)
        ga_tmp = z_gate[:, 0, :].rearrange("p (t h) -> p t h", h=H)
        b_rep = sb("b_rep", [P, HALVES, T])
        c_repl = sb("c_repl", [P, HALVES, T])
        d_bu = sb("d_bu", [P, 2, 2, T])
        states = sb("states", [P, HALVES, DB, T])
        prod = sb("prod", [P, 2, 2, T])
        carry = sb("carry", [P, DB, N])
        w_gu = sb("w_gu", [P, SLOTS, GU])
        w_down = sb("w_down", [P, SLOTS, H])
        w_rep = sb("w_rep", [P, SLOTS, T])
        d_diag = w_rep[:, :, 0:P]
        act = sb("act", [P, 2, T])
        inter = sb("inter", [P, 2, T])
        d_bu_shared = inter
        o_fm = tmp_b[:, 0:KH, :]
        logits = sb("logits", [P, TT, E + 1])
        top8 = sb("top8", [P, TT, 8])
        knocked = x_norm[:, :, 0:E]
        neg_max = sb("neg_max", [P, TT])
        e_val = x_norm[:, :, E:2 * E]
        sh_th = sb("sh_th", [P, TT, 1])
        e_sum = sb("e_sum", [P, TT])
        w_tok = sb("w_tok", [P, TT, E + 2])
        w_fm = sb("w_fm", [E + 2, T])

        bc_dram = [nc.dram_tensor(f"bc_scratch{i}", (2 * N, T), fp32, kind="Internal").ap() for i in range(2)]
        w_dram = [nc.dram_tensor(f"w_scratch{i}", (E + 2, T), fp32, kind="Internal").ap() for i in range(2)]

        bank = [ctx.enter_context(nc.psum_tensor(f"bank{i}", [P, T], fp32)) for i in range(8)]
        gate_ps, up_ps, out_ps = bank[0:2], bank[2:4], bank[4:6]

        def da_banks(p, i):
            return 2 if p == 0 or isinstance(i, int) and i == 0 else 1

        def da_bank(p, i, e):
            if da_banks(p, i) == 1 or e == 0:
                return bank[6]
            return bank[7] if p == 0 else bank[1]

        def piece_bank(index):
            if index < ROUND + PIECES:
                return bank[4 + index % 2]
            return bank[4] if index % ROUND >= PIECES and index % 2 else bank[7]

        def pieces_in_flight(index):
            return 1 if index < ROUND + PIECES or index % ROUND > PIECES else 0

        logits_ps, w_ps = bank[3], bank[5]
        out_t_ps = (bank[0], bank[2])

        cond_in = sem("cond_in")
        conv_in = sem("conv_in")
        weights_in = sem("weights_in")
        waits_passed = sem("waits_passed")
        ident_ready = sem("ident_ready")
        dve_setup = sem("dve_setup")
        dve_setup_steps = sem("dve_setup_steps")
        silu_c_th = sem("silu_c_th")
        silu_c_rep = sem("silu_c_rep")
        mod_ready = sem("mod_ready")
        setup_done = sem("setup_done")
        zeros_ready = sem("zeros_ready")
        a_ready = sem("a_ready")
        x_arrived = sem("x_arrived")
        x_free = sem("x_free")
        dve_pre = sem("dve_pre")
        dve_post = sem("dve_post")
        xn_ready = sem("xn_ready")
        xn2_ready = sem("xn2_ready")
        xn2T_ready = sem("xn2T_ready")
        piece_ready = sem("piece_ready")
        piece_read = sem("piece_read")
        z_ready = sem("z_ready")
        z_done = sem("z_done")
        hist_saved = sem("hist_saved")
        tap_ready = sem("tap_ready")
        conv_ready = sem("conv_ready")
        u_th_ready = sem("u_th_ready")
        u_ready = sem("u_ready")
        y_started = sem("y_started")
        bc_written = sem("bc_written")
        abs_ready = sem("abs_ready")
        series_ready = sem("series_ready")
        e_ready = sem("e_ready")
        log_ready = sem("log_ready")
        dt_ready = sem("dt_ready")
        dtu_ready = sem("dtu_ready")
        b_arrived = [sem(f"b_arrived{i}") for i in range(HALVES)]
        c_arrived = [sem(f"c_arrived{i}") for i in range(HALVES)]
        dbu_shared = sem("dbu_shared")
        dbu_done = [sem(f"dbu_done{i}") for i in range(HALVES)]
        da_ready = sem("da_ready")
        scan_done = sem("scan_done")
        prod_done = [sem(f"prod_done{i}") for i in range(HALVES)]
        acc_done = sem("acc_done")
        summed = [sem(f"summed{i}") for i in range(2)]
        carry_saved = [sem(f"carry_saved{i}") for i in range(HALVES)]
        gu_arrived = [sem(f"gu_arrived{i}") for i in range(SLOTS)]
        down_arrived = [sem(f"down_arrived{i}") for i in range(SLOTS)]
        wrep_arrived = [sem(f"wrep_arrived{i}") for i in range(SLOTS)]
        pair_done = [sem(f"pair_done{i}") for i in range(SLOTS)]
        gate_ready = sem("gate_ready")
        up_ready = sem("up_ready")
        th_ready = sem("th_ready")
        act_ready = sem("act_ready")
        product_ready = sem("product_ready")
        inter_ready = sem("inter_ready")
        moe_ready = sem("moe_ready")
        o_ready = sem("o_ready")
        ofm_ready = sem("ofm_ready")
        oT_ready = sem("oT_ready")
        out_ready = sem("out_ready")
        stored = sem("stored")
        gated = sem("gated")
        attn_ready = sem("attn_ready")
        logits_ready = sem("logits_ready")
        negmax_ready = sem("negmax_ready")
        e_val_ready = sem("e_val_ready")
        wtok_ready = sem("wtok_ready")
        wT_ready = sem("wT_ready")
        w_fm_ready = sem("w_fm_ready")
        w_written = sem("w_written")
        block = ctx.enter_context(nc.Block())

        def wait_alone(eng, signal, value):
            eng.wait_ge(signal, value)
            eng.sem_inc(waits_passed, 1)

        SA, CA, GA, SB, CB, GB = range(6)

        def col(j, k):
            return mod_col[:, j * KH + k:j * KH + k + 1]

        def wmod_sb(k):
            return (y, dtu)[k][:].rearrange("p d t -> p (d t)")[:, 0:6 * H]

        NLOAD = 16 * (KH + 7)

        def is_shared(j):
            return isinstance(j, int) and j == PAIRS - 1

        def rows_of(j):
            return slice(0, SH) if is_shared(j) else slice(0, P)

        def at_quarters(eng, p, quarter, piece):
            first = BODIES if p < CH - 1 else LAST_BODIES
            for k in range(first * SLOTS):
                quarter(k // SLOTS, k % SLOTS)
                piece(k)
            if first < BODIES:
                with eng.Fori(first, BODIES) as i:
                    for c in range(SLOTS):
                        quarter(i, c)

        @block.sync
        def _(sp):
            sp.sem_inc(stored, FREE)
            sp.dma_start(c_col[:], cond).then_inc(cond_in, 16)
            for k in range(KH):
                sp.dma_start(wmod_sb(k)[:, 0:2 * H], wmod[:, k, 0:2 * H]).then_inc(cond_in, 16)
            sp.dma_start(x_tok[0][:], x_in[0:T, :].rearrange("(t p) h -> p t h", p=P)).then_inc(x_arrived, 16)
            for dst, src in [(w_conv, conv_w), (b_conv, conv_b), (w_in, in_proj)]:
                sp.dma_start(dst[:], src).then_inc(conv_in, 16)
            for dst, src in [(w_xp, x_proj), (w_dt, dt_proj), (b_dt, dt_b), (a_neg, a_log), (d_sk, d_skip)]:
                sp.dma_start(dst[:], src).then_inc(weights_in, 16)
            for k in range(KH):
                sp.dma_start(wmod_sb(k)[:, 2 * H:], wmod[:, k, 2 * H:]).then_inc(weights_in, 16)
            for dst, src in [(w_out, out_proj), (w_rt, router)]:
                sp.dma_start(dst[:], src).then_inc(weights_in, 16)

            def load_x(c):
                if c >= 2:
                    sp.wait_ge(x_free, (c - 1) * (TT // 2))
                sp.dma_start(x_tok[c % 2][:], x_in[bass.ts(c, T), :].rearrange("(t p) h -> p t h", p=P)) \
                    .then_inc(x_arrived, 16)

            def write_bc(c):
                sp.wait_ge(piece_read, c * ROUND + PIECES)
                sp.dma_start(bc_dram[c % 2], bc_low[:]).then_inc(bc_written, 16)

            def load_b(p, i, hf):
                wait_alone(sp, dbu_done[hf], (i + p * BODIES) * 2 + FREE)
                sp.dma_start(b_rep[:, hf, :], bc_dram[p % 2][bass.ds(i * HALVES + hf, 1), :].to_broadcast([P, T])) \
                    .then_inc(b_arrived[hf], 16)

            def load_c(p, i, hf):
                wait_alone(sp, prod_done[hf], (i + p * BODIES) * 2 + FREE)
                sp.dma_start(c_repl[:, hf, :],
                             bc_dram[p % 2][bass.ds(i * HALVES + hf + N, 1), :].to_broadcast([P, T])) \
                    .then_inc(c_arrived[hf], 16)

            def load_gate_up(m, j, s):
                if not isinstance(j, int) or j >= SLOTS:
                    sp.wait_ge(up_ready, j - SLOTS + m * PAIRS + 1)
                elif m > 0:
                    sp.wait_ge(up_ready, m * PAIRS - (SLOTS - j) % SLOTS)
                sp.dma_start(w_gu[:, s, :], pair_w[bass.ds(j, 1), :, 0:GU].rearrange("a p n -> (a p) n")) \
                    .then_inc(gu_arrived[s], 16)

            def load_down(m, j, s, before):
                wait_alone(sp, pair_done[s], m * LOADS[s] + before + FREE)
                sp.dma_start(w_down[:, s, :], pair_w[bass.ds(j, 1), :, GU:].rearrange("a p n -> (a p) n")) \
                    .then_inc(down_arrived[s], 16)

            def load_routing(m, j, s):
                for e in range(2):
                    sp.dma_start(w_rep[64 * e:64 * e + 64, s, :],
                                 w_dram[m % 2][bass.ds(j * 2 + e, 1), :].to_broadcast([64, T])) \
                        .then_inc(wrep_arrived[s], 16)

            def store(m):
                sp.wait_ge(out_ready, (m + 1) * (TT // 2))
                sp.dma_start(out[bass.ts(m, T), :].rearrange("(t p) h -> p t h", p=P), x_mid[m % 2][:]) \
                    .then_inc(stored, 16)

            write_bc(0)
            for p in range(CH + 1):
                m = p - 1
                scan, moe = p < CH, p > 0
                if p + 1 < CH:
                    load_x(p + 1)
                if scan:
                    sp.wait_ge(bc_written, 16 * (p + 1))

                def quarter(i, c):
                    if scan and c % 2 == 0:
                        load_b(p, i, c // 2)
                    if moe and isinstance(i, int) and i == 1 and c == 0:
                        sp.wait_ge(w_written, 16 * (m + 1))
                        for j in range(SLOTS):
                            load_routing(m, j, j)
                    if scan and c % 2 == 0:
                        load_c(p, i, c // 2)
                    if moe and not (isinstance(i, int) and i <= 1):
                        t = (c + 1) % SLOTS
                        j = (i - 1) * SLOTS + c
                        load_gate_up(m, j + 3, (c + 3) % SLOTS)
                        load_down(m, j + 1, t, i - 1 + (1 if t == 0 else 0))
                        load_routing(m, j + 1, t)

                def piece(k):
                    if k == 26 and p + 1 < CH:
                        write_bc(p + 1)
                    if moe:
                        if k == 1:
                            for j in (1, 2, 3, 0):
                                load_gate_up(m, j, j)
                            for j in (1, 2, 3, 0):
                                load_down(m, j, j, 0)
                        elif k == 2 and m >= 1:
                            store(m - 1)
                        elif SLOTS < k < 2 * SLOTS:
                            load_gate_up(m, k - SLOTS + 3, (k + 3) % SLOTS)
                            if k == 2 * SLOTS - 1:
                                load_down(m, SLOTS, 0, 1)
                                load_routing(m, SLOTS, 0)

                at_quarters(sp, p, quarter, piece)
                if moe:
                    for j in range(PAIRS - LATE + 1, PAIRS):
                        if j + 2 < PAIRS:
                            load_gate_up(m, j + 2, (j + 2) % SLOTS)
                        load_down(m, j, j % SLOTS, j // SLOTS)
                        load_routing(m, j, j % SLOTS)
            store(CH - 1)
            sp.wait_ge(stored, 16 * CH + FREE)
            sp.wait_ge(w_written, 16 * CH)
            sp.wait_ge(bc_written, 16 * CH)

        @block.gpsimd
        def _(pool):
            for signal in prod_done + carry_saved:
                pool.sem_inc(signal, FREE)
            nc.gpsimd.memset(ident[:], 0.0).then_inc(ident_ready, 1)
            pool.wait_ge(ident_ready, 1)
            nc.gpsimd.affine_select(out=ident[:], in_=ident[:], compare_op=ALU.not_equal, fill=1.0, base=0,
                                    pattern=[[-1, P]], channel_multiplier=1).then_inc(ident_ready, 1)

            def make_dtu(p):
                if p > 0:
                    for signal in dbu_done:
                        pool.wait_ge(signal, p * QUARTERS // HALVES + FREE)
                for half in range(2):
                    blocks = slice(2 * half, 2 * half + 2)
                    pool.wait_ge(dt_ready, p * 2 + half + 1)
                    nc.gpsimd.tensor_tensor(dtu[:, blocks, :], dt[p % 2][:, blocks, :], u[:, blocks, :],
                                            ALU.mult).then_inc(dtu_ready, 1)

            def quarter(p, i, c):
                g, hf, r = i + p * BODIES, c // 2, c % 2
                if r == 0:
                    pool.wait_ge(c_arrived[hf], (g + 1) * 16)
                if p == 0:
                    pool.wait_ge(summed[r], g * 2 + hf + FREE)
                pool.wait_ge(scan_done, g * 2 * SLOTS + 2 * c + 2 + 2 * FREE)
                nc.gpsimd.tensor_tensor(prod[:, r], states[:, hf, 2 * r:2 * r + 2, :],
                                        c_repl[:, hf:hf + 1, :].to_broadcast([P, 2, T]),
                                        ALU.mult).then_inc(prod_done[hf], 1)
                if r == 1:
                    nc.gpsimd.tensor_copy(carry[:, :, bass.ds(i * HALVES + hf, 1)],
                                          states[:, hf, :, T - 1:T]).then_inc(carry_saved[hf], 1)
                if p > 0:
                    pool.wait_ge(y_started, p)
                    pool.wait_ge(prod_done[hf], g * 2 + r + 1 + FREE)
                    nc.gpsimd.tensor_tensor(y[:, 2 * r:2 * r + 2, :], y[:, 2 * r:2 * r + 2, :], prod[:, r],
                                            ALU.add).then_inc(acc_done, 1)

            def shared_inputs(i):
                pool.wait_ge(b_arrived[1], (i + 1) * 16)
                pool.wait_ge(scan_done, i * 2 * SLOTS + 2 * FREE)
                nc.gpsimd.tensor_tensor(d_bu_shared[:], dtu[:, 2:4, :],
                                        b_rep[:, 1:2, :].to_broadcast([P, 2, T]), ALU.mult) \
                    .then_inc(dbu_shared, 1)

            make_dtu(0)
            pool.wait_ge(dtu_ready, 2)
            with pool.Fori(0, SHARED) as i:
                for c in range(SLOTS):
                    if c == 1:
                        shared_inputs(i)
                    quarter(0, i, c)
            for i in range(SHARED, BODIES):
                for c in range(SLOTS):
                    quarter(0, i, c)
            for p in range(1, CH):
                make_dtu(p)
                with pool.Fori(0, BODIES) as i:
                    for c in range(SLOTS):
                        quarter(p, i, c)

        @block.scalar
        def _(sca):
            sca.wait_ge(cond_in, 16 * (KH + 1))
            nc.scalar.activation(c_th[:], c_col[:], ACT.Tanh, scale=0.5).then_inc(silu_c_th, 1)
            sca.wait_ge(dve_setup, 1)

            def modulate(dst, ps, cj, sj, k, done):
                nc.scalar.activation(dst[:, k, :], ps[:], ACT.Identity, bias=col(sj, k), scale=col(cj, k)) \
                    .then_inc(done, 1)

            def gate_piece(p, k):
                if 1 <= k < 1 + DB:
                    b = k - 1
                    index = p * ROUND + PIECES + b
                    if b == 0:
                        sca.wait_ge(dt_ready, (p + 1) * 2)
                        if p > 0:
                            sca.wait_ge(attn_ready, p * (TT // 2))
                    sca.wait_ge(piece_ready, index + 1)
                    nc.scalar.activation(z_gate[:, b, :], piece_bank(index)[:], ACT.Copy).then_inc(z_ready, 1)
                    nc.scalar.activation(tmp_c[:, b, :], piece_bank(index)[:], ACT.Tanh, scale=0.5) \
                        .then_inc(piece_read, 1)

            def pre_piece(c, k):
                first = c * ROUND
                if 6 <= k < 6 + KH:
                    index = first + k - 6
                    sca.wait_ge(piece_ready, index + 1)
                    modulate(h_attn, piece_bank(index), CA, SA, k - 6, piece_read)
                elif 9 <= k < 9 + DB:
                    b = k - 9
                    index = first + KH + b
                    sca.wait_ge(piece_ready, index + 1)
                    sca.wait_ge(hist_saved, c + 1)
                    nc.scalar.activation(tmp_a[:, b, :], piece_bank(index)[:], ACT.Identity,
                                         bias=b_conv[:, b:b + 1], scale=w_conv[:, b, TAPS - 1:TAPS]) \
                        .then_inc(tap_ready, 1)
                    nc.scalar.activation(u_raw[:, b, TAPS - 1:], piece_bank(index)[:], ACT.Copy) \
                        .then_inc(piece_read, 1)
                elif k == 18:
                    index = first + KH + DB
                    sca.wait_ge(piece_ready, index + 1)
                    nc.scalar.activation(dt_low[:], piece_bank(index)[:], ACT.Copy).then_inc(piece_read, 1)
                elif 20 <= k < 20 + DB:
                    b = k - 20
                    index = first + KH + DB + 1 + b
                    sca.wait_ge(piece_ready, index + 1)
                    nc.scalar.activation(tmp_a[:, b, :], piece_bank(index)[:], ACT.Abs,
                                         bias=b_dt[:, b:b + 1]).then_inc(abs_ready, 1)
                    nc.scalar.activation(dt[c % 2][:, b, :], piece_bank(index)[:], ACT.Identity,
                                         bias=b_dt[:, b:b + 1]).then_inc(piece_read, 1)
                    sca.wait_ge(abs_ready, c * DB + b + 1)
                    nc.scalar.activation(tmp_a[:, b, :], tmp_a[:, b, :], ACT.Exp, scale=-1.0).then_inc(e_ready, 1)
                    sca.wait_ge(e_ready, c * DB + b + 1)
                    nc.scalar.activation(tmp_c[:, b, :], tmp_a[:, b, :], ACT.Square, scale=3.0 ** -0.5,
                                         bias=root_bias[:]).then_inc(series_ready, 1)
                elif k == 24:
                    index = first + PIECES - 1
                    if c > 0:
                        sca.wait_ge(bc_written, 16 * c)
                    sca.wait_ge(piece_ready, index + 1)
                    nc.scalar.activation(bc_low[:], piece_bank(index)[0:2 * N, :], ACT.Copy) \
                        .then_inc(piece_read, 1)
                elif k == LOGS:
                    for half in range(2):
                        blocks = slice(2 * half, 2 * half + 2)
                        nc.scalar.activation(tmp_b[:, blocks, :], tmp_a[:, blocks, :], ACT.Ln, bias=1.0) \
                            .then_inc(log_ready, 1)
                if 11 <= k < 11 + DB:
                    b = k - 11
                    sca.wait_ge(conv_ready, c * DB + b + 1)
                    nc.scalar.activation(tmp_b[:, b, :], tmp_a[:, b, :], ACT.Tanh).then_inc(u_th_ready, 1)

            def decay(p, i, c, e):
                unit = (i + p * BODIES) * 2 * SLOTS + 2 * c + e
                d = 2 * (c % 2) + e
                sca.wait_ge(scan_done, unit - da_banks(p, i) + 1 + 2 * FREE)
                nc.scalar.activation(da_bank(p, i, e)[:], dt[p % 2][:, d, :], ACT.Exp,
                                     scale=a_neg[:, d, bass.ds(i * HALVES + c // 2, 1)]).then_inc(da_ready, 1)

            def pair_tanh(m, j, q):
                sca.wait_ge(inter_ready, j + m * PAIRS - 1 + 2 * FREE)
                sca.wait_ge(up_ready if is_shared(j) else gate_ready, j + m * PAIRS + 1)
                rows = rows_of(j)
                nc.scalar.activation(act[rows, q, :], gate_ps[q][rows, :], ACT.Tanh, scale=0.5).then_inc(th_ready, 1)

            def outputs(m):
                for k in range(KH):
                    sca.wait_ge(o_ready, m * KH + k + 1)
                    nc.scalar.activation(o_fm[:, k, :], out_ps[k][:], ACT.Copy,
                                         scale=gb_col[:, k:k + 1]).then_inc(ofm_ready, 1)

            def router(p, k):
                if k == 0:
                    sca.wait_ge(negmax_ready, p + 1)
                    for t in range(TT):
                        nc.scalar.activation(e_val[:, t, :], logits[:, t, 0:E], ACT.Exp,
                                             bias=neg_max[:, t:t + 1])
                    nc.scalar.activation(sh_th[:], logits[:, :, E:E + 1], ACT.Tanh, scale=0.5) \
                        .then_inc(e_val_ready, 1)
                elif k == 2:
                    sca.wait_ge(wT_ready, p + 1)
                    if p > 0:
                        sca.wait_ge(w_written, 16 * p)
                    nc.scalar.activation(w_fm[:], w_ps[0:E + 2, :], ACT.Copy).then_inc(w_fm_ready, 1)
                    sca.wait_ge(w_fm_ready, p + 1)
                    sca.dma_start(w_dram[p % 2], w_fm[:]).then_inc(w_written, 16)

            for k in range(QUARTERS):
                if k == 16:
                    sca.wait_ge(weights_in, NLOAD)
                    nc.scalar.activation(a_neg[:], a_neg[:], ACT.Exp).then_inc(a_ready, 1)
                pre_piece(0, k)
            sca.wait_ge(setup_done, 1)
            for p in range(CH + 1):
                scan, moe = p < CH, p > 0
                m = p - 1

                def quarter(i, c):
                    if scan:
                        decay(p, i, c, 0)
                    if moe and not (isinstance(i, int) and i == 0):
                        pair_tanh(m, (i - 1) * SLOTS + c, c % 2)
                    if scan:
                        decay(p, i, c, 1)

                def piece(k):
                    if scan and moe and k == 0:
                        sca.wait_ge(gated, p)
                        for b in range(DB):
                            last = nc.scalar.activation(y[:, b, :], u[:, b, :], ACT.Copy,
                                                        scale=d_sk[:, b:b + 1])
                        last.then_inc(y_started, 1)
                    if moe:
                        router(m, k)
                    if scan:
                        gate_piece(p, k)
                    if p + 1 < CH and (moe or k != LOGS + 1):
                        pre_piece(p + 1, k - 1)

                if scan:
                    sca.wait_ge(dt_ready, (p + 1) * 2)
                    if moe:
                        sca.wait_ge(moe_ready, p * KH)
                at_quarters(sca, p, quarter, piece)
                if not moe:
                    pre_piece(1, LOGS)
                if moe:
                    for j in range(PAIRS - LATE, PAIRS):
                        pair_tanh(m, j, j % 2)
                if scan:
                    for k in range(KH):
                        sca.wait_ge(xn2T_ready, p * KH + k + 1)
                        modulate(h_moe, bank[6 + k], CB, SB, k, moe_ready)
                if moe:
                    outputs(m)

        @block.vector
        def _(dve):
            v = nc.vector

            def steps(counted, base):
                count = [base]

                def step(ins):
                    ins.then_inc(counted, 1)
                    count[0] += 1

                def sync():
                    dve.wait_ge(counted, count[0])

                return step, sync

            step, sync = steps(dve_setup_steps, 0)
            pre_step, pre_sync = steps(dve_pre, 0)
            post_step, post_sync = steps(dve_post, 0)

            def norm_stats(step, sync, src):
                for t in range(TT):
                    step(v.bn_stats(stats[:, t, :], src[:, t, :]))
                sync()
                for t in range(TT):
                    step(v.bn_aggr(mean_var[:, t, :], stats[:, t, :]))
                sync()

            def norm_root(step, sync):
                step(v.tensor_scalar(var_eps[:], mean_var[:, :, 1], EPS, None, ALU.add))
                sync()
                step(v.tensor_scalar(newton[:].bitcast(i32), var_eps[:].bitcast(i32), 1, None,
                                     ALU.arith_shift_right))
                sync()
                step(v.tensor_scalar(rstd[:].bitcast(i32), newton[:].bitcast(i32), -1.0, float(0x5F3759DF),
                                     ALU.mult, ALU.add))
                sync()
                for _ in range(3):
                    step(v.tensor_tensor(newton[:], rstd[:], rstd[:], ALU.mult))
                    sync()
                    step(v.scalar_tensor_tensor(newton[:], newton[:], -0.5, var_eps[:], ALU.mult, ALU.mult))
                    sync()
                    step(v.scalar_tensor_tensor(rstd[:], newton[:], 1.5, rstd[:], ALU.add, ALU.mult))
                    sync()

            def norm_apply(src, ready):
                for t in range(TT):
                    last = v.tensor_scalar(x_norm[:, t, :], src[:, t, :], mean_var[:, t, 0:1], rstd[:, t:t + 1],
                                           ALU.subtract, ALU.mult)
                last.then_inc(ready, 1)

            def setup():
                for signal in dbu_done:
                    dve.sem_inc(signal, FREE)
                dve.sem_inc(scan_done, 2 * FREE)
                dve.sem_inc(inter_ready, 2 * FREE)
                v.memset(zeros_bf[:], 0.0).then_inc(zeros_ready, 1)
                step(v.memset(carry[:], 0.0))
                step(v.memset(u_raw[:, :, T:T + TAPS - 1], 0.0))
                step(v.memset(root_bias[:], -(3.0 ** 0.5) / 4.0))
                step(v.memset(ones[:], 1.0))
                dve.wait_ge(silu_c_th, 1)
                step(v.scalar_tensor_tensor(c_col[:], c_th[:], 1.0, c_col[:], ALU.add, ALU.mult))
                sync()
                step(v.tensor_scalar(c_col[:], c_col[:], 0.5, None, ALU.mult))
                sync()
                for k in range(KH):
                    last = v.tensor_scalar(c_rep[:, k, :], ones[:], c_col[:, k:k + 1], None, ALU.mult)
                last.then_inc(silu_c_rep, 1)

            def setup_attention():
                dve.wait_ge(mod_ready, 1)
                v.tensor_copy(mod_col[:, SA * KH:SA * KH + KH], gate_ps[0][:, SA * KH:SA * KH + KH])
                step(v.tensor_scalar(mod_col[:, CA * KH:CA * KH + KH], gate_ps[0][:, CA * KH:CA * KH + KH],
                                     1.0, None, ALU.add))
                sync()
                dve.wait_ge(conv_in, 16 * 3)
                step(v.tensor_scalar(w_conv[:], w_conv[:], 0.5, None, ALU.mult))
                step(v.tensor_scalar(b_conv[:], b_conv[:], 0.5, None, ALU.mult))
                sync()
                dve.sem_inc(dve_setup, 1)

            def setup_rest():
                step(v.memset(w_tok[:], 0.0))
                dve.wait_ge(a_ready, 1)
                dve.wait_ge(ident_ready, 2)
                for b in range(DB):
                    step(v.tensor_scalar(d_diag[:, b, :], ident[:], d_sk[:, b:b + 1], None, ALU.mult))
                step(v.tensor_scalar(a_neg[:], a_neg[:], -1.0, None, ALU.mult))
                dve.wait_ge(mod_ready, 2)
                step(v.tensor_copy(mod_col[:, GA * KH:], gate_ps[0][:, GA * KH:6 * KH]))
                step(v.tensor_copy(ga_row[:, 0, :], gate_ps[1][:, 0:H]))
                step(v.tensor_copy(ga_row[:, 1, :], gate_ps[1][:, 0:H]))
                sync()
                step(v.tensor_scalar(mod_col[:, CB * KH:CB * KH + KH], mod_col[:, CB * KH:CB * KH + KH],
                                     1.0, None, ALU.add))
                g_col = mod_col[:, GB * KH:GB * KH + KH]
                for g, tmp, dst in ((ga_row[:], ga_tmp, ga_row[:]), (g_col, gb_tmp[:], gb_col[:])):
                    step(v.tensor_scalar(tmp, g, 0.0, 2.0, ALU.is_ge, ALU.mult))
                    sync()
                    step(v.scalar_tensor_tensor(dst, g, -1.0, g, ALU.mult, ALU.max))
                    sync()
                    step(v.tensor_scalar(dst, dst, 0.25, None, ALU.max))
                    sync()
                    step(v.scalar_tensor_tensor(dst, tmp, -1.0, dst, ALU.add, ALU.mult))
                sync()
                dve.sem_inc(setup_done, 1)

            def gate_piece(p, k):
                if 5 <= k < 5 + DB:
                    b = k - 5
                    dve.wait_ge(piece_read, p * ROUND + PIECES + b + 1)
                    v.scalar_tensor_tensor(z_gate[:, b, :], tmp_c[:, b, :], 1.0, z_gate[:, b, :],
                                           ALU.add, ALU.mult).then_inc(z_done, 1)

            def pre_piece(c, k):
                x = x_tok[c % 2]
                dtc = dt[c % 2]
                if k == 1:
                    v.tensor_copy(u_raw[:, :, 0:TAPS - 1], u_raw[:, :, T:T + TAPS - 1]).then_inc(hist_saved, 1)
                elif k == 2:
                    dve.wait_ge(x_arrived, (c + 1) * 16)
                    norm_stats(pre_step, pre_sync, x)
                elif k == 3:
                    norm_root(pre_step, pre_sync)
                elif k == 4:
                    norm_apply(x, xn_ready)
                if 10 <= k < 10 + DB:
                    b = k - 10
                    dve.wait_ge(piece_read, c * ROUND + KH + b + 1)
                    dve.wait_ge(tap_ready, c * DB + b + 1)
                    for tap in range(TAPS - 1):
                        ins = v.scalar_tensor_tensor(tmp_a[:, b, :], u_raw[:, b, tap:tap + T],
                                                     w_conv[:, b, tap:tap + 1], tmp_a[:, b, :],
                                                     ALU.mult, ALU.add)
                        if tap < TAPS - 2:
                            pre_step(ins)
                            pre_sync()
                        else:
                            ins.then_inc(conv_ready, 1)
                if 12 <= k < 12 + DB:
                    b = k - 12
                    dve.wait_ge(u_th_ready, c * DB + b + 1)
                    v.scalar_tensor_tensor(u[:, b, :], tmp_b[:, b, :], 1.0, tmp_a[:, b, :], ALU.add, ALU.mult) \
                        .then_inc(u_ready, 1)
                series, at = (tmp_c, 24) if c == 0 else (tmp_a, 26)
                if k in (at, at + 1):
                    half = k - at
                    blocks = slice(2 * half, 2 * half + 2)
                    dve.wait_ge(series_ready, c * DB + 2 * half + 2)
                    if c > 0:
                        dve.wait_ge(log_ready, c * 2 + half + 1)
                    pre_step(v.tensor_scalar(small_e[:, blocks, :], tmp_a[:, blocks, :], TINY, None, ALU.is_lt))
                    pre_sync()
                    pre_step(v.scalar_tensor_tensor(series[:, blocks, :], tmp_c[:, blocks, :], 13.0 / 16.0,
                                                    tmp_a[:, blocks, :], ALU.add, ALU.mult))
                if 27 <= k < 31:
                    half = (k - 27) // 2
                    blocks = slice(2 * half, 2 * half + 2)
                    if k in (27, 29):
                        dve.wait_ge(log_ready, c * 2 + half + 1)
                        pre_sync()
                        pre_step(v.copy_predicated(tmp_b[:, blocks, :], small_e[:, blocks, :], series[:, blocks, :]))
                    else:
                        pre_sync()
                        v.scalar_tensor_tensor(dtc[:, blocks, :], dtc[:, blocks, :], 0.0, tmp_b[:, blocks, :],
                                               ALU.max, ALU.add).then_inc(dt_ready, 1)

            def inputs(p, i, c):
                g, hf, r = i + p * BODIES, c // 2, c % 2
                dve.wait_ge(dtu_ready, p * 2 + r + 1)
                if p == 0 and c == SLOTS - 1 and i < SHARED:
                    dve.wait_ge(dbu_shared, i + 1)
                    dve.sem_inc(dbu_done[hf], 1)
                    return
                if r == 0:
                    dve.wait_ge(b_arrived[hf], (g + 1) * 16)
                if p > 0 or i > 0 or c > 1:
                    dve.wait_ge(scan_done, g * 2 * SLOTS + 2 * c - 2 + 2 * FREE)
                v.tensor_tensor(d_bu[:, r], dtu[:, 2 * r:2 * r + 2, :],
                                b_rep[:, hf:hf + 1, :].to_broadcast([P, 2, T]), ALU.mult) \
                    .then_inc(dbu_done[hf], 1)

            def unit(p, i, c, e):
                g, hf, r = i + p * BODIES, c // 2, c % 2
                d = 2 * r + e
                if r == 0 and e == 0:
                    dve.wait_ge(prod_done[hf], g * 2 + FREE)
                    dve.wait_ge(carry_saved[hf], g + FREE)
                if e == 0:
                    dve.wait_ge(dbu_done[hf], g * 2 + r + 1 + FREE)
                dve.wait_ge(da_ready, g * 2 * SLOTS + 2 * c + e + 1)
                d_input = d_bu_shared if p == 0 and c == SLOTS - 1 and i < SHARED else d_bu[:, r]
                v.tensor_tensor_scan(states[:, hf, d, :], da_bank(p, i, e)[:], d_input[:, e, :],
                                     carry[:, d, bass.ds(i * HALVES + hf, 1)], ALU.mult, ALU.add) \
                    .then_inc(scan_done, 1)

            def pair_gate(m, j, q):
                dve.wait_ge(th_ready, j + m * PAIRS + 1)
                rows = rows_of(j)
                v.scalar_tensor_tensor(act[rows, q, :], act[rows, q, :], 1.0, gate_ps[q][rows, :], ALU.add, ALU.mult) \
                    .then_inc(act_ready, 1)

            def pair_up(m, j, q):
                dve.wait_ge(up_ready, j + m * PAIRS + 1)
                dve.wait_ge(act_ready, j + m * PAIRS + 1)
                rows = rows_of(j)
                up = gate_ps[q][SH:2 * SH, :] if is_shared(j) else up_ps[q][:]
                v.tensor_tensor(up_ps[q][rows, :], act[rows, q, :], up, ALU.mult).then_inc(product_ready, 1)

            def pair_weigh(m, j, s, arrivals):
                q = s % 2
                dve.wait_ge(wrep_arrived[s], (arrivals + m * LOADS[s]) * 32)
                dve.wait_ge(product_ready, j + m * PAIRS + 1)
                o = (s + 2) % SLOTS
                dve.wait_ge(pair_done[o], arrivals + m * LOADS[o] - (1 if s < 2 else 0) + FREE)
                rows = rows_of(j)
                v.tensor_tensor(inter[rows, q, :], up_ps[q][rows, :], w_rep[rows, s, :], ALU.mult).then_inc(inter_ready, 1)

            def finish(m):
                x = x_mid[m % 2]
                for k in range(TT // 2):
                    dve.wait_ge(oT_ready, m * (TT // 2) + k + 1)
                    v.tensor_tensor(x[:, 2 * k:2 * k + 2, :], x[:, 2 * k:2 * k + 2, :],
                                    out_t_ps[k][:].rearrange("p (t h) -> p t h", h=H), ALU.add) \
                        .then_inc(out_ready, 1)

            def gating(p):
                if p == 0:
                    for r in range(2):
                        dve.wait_ge(summed[r], QUARTERS // 2 + FREE)
                else:
                    dve.wait_ge(acc_done, p * QUARTERS)
                for b in range(DB):
                    last = v.scalar_tensor_tensor(tmp_c[:, b, :], bank[b][:] if p == 0 else y[:, b, :], 0.5,
                                                  z_gate[:, b, :], ALU.mult, ALU.mult)
                last.then_inc(gated, 1)

            def residual(p):
                x = x_mid[p % 2]
                if p >= 2:
                    dve.wait_ge(stored, (p - 1) * 16 + FREE)
                for k in range(TT // 2):
                    tiles = slice(2 * k, 2 * k + 2)
                    dve.wait_ge(attn_ready, p * (TT // 2) + k + 1)
                    post_step(v.tensor_tensor(x[:, tiles, :], bank[6 + k][:].rearrange("p (t h) -> p t h", h=H),
                                              ga_row[:], ALU.mult))
                    post_sync()
                    v.tensor_tensor(x[:, tiles, :], x[:, tiles, :], x_tok[p % 2][:, tiles, :], ALU.add) \
                        .then_inc(x_free, 1)
                    dve.wait_ge(x_free, p * (TT // 2) + k + 1)
                    for t in (2 * k, 2 * k + 1):
                        post_step(v.bn_stats(stats[:, t, :], x[:, t, :]))
                post_sync()
                for t in range(TT):
                    post_step(v.bn_aggr(mean_var[:, t, :], stats[:, t, :]))
                post_sync()
                norm_root(post_step, post_sync)
                norm_apply(x, xn2_ready)

            def router(p, k):
                if k == 0:
                    dve.wait_ge(logits_ready, p + 1)
                    post_step(v.tensor_copy(logits[:].rearrange("p t e -> p (t e)"),
                                            logits_ps[:, 0:TT * (E + 1)]))
                    post_sync()
                    for t in range(TT):
                        post_step(v.max(top8[:, t, :], logits[:, t, 0:E]))
                    post_sync()
                    v.tensor_scalar(neg_max[:], top8[:, :, 0], -1.0, None, ALU.mult).then_inc(negmax_ready, 1)
                    for t in range(TT):
                        post_step(v.match_replace(knocked[:, t, :], top8[:, t, :], logits[:, t, 0:E], -3.0e38))
                    post_sync()
                    post_step(v.tensor_tensor(knocked, knocked, logits[:, :, 0:E], ALU.not_equal))
                elif k == 1:
                    dve.wait_ge(e_val_ready, p + 1)
                    post_sync()
                    post_step(v.tensor_tensor(e_val, e_val, knocked, ALU.mult))
                    post_step(v.tensor_scalar(w_tok[:, :, E:E + 1], sh_th[:], 1.0, 0.25, ALU.add, ALU.mult))
                    post_sync()
                    post_step(v.tensor_reduce(e_sum[:], e_val, AX.X, ALU.add))
                    post_sync()
                    post_step(v.reciprocal(e_sum[:], e_sum[:]))
                    post_sync()
                    for t in range(TT):
                        last = v.tensor_scalar(w_tok[:, t, 0:E], e_val[:, t, :], e_sum[:, t:t + 1], 0.5,
                                               ALU.mult, ALU.mult)
                    last.then_inc(wtok_ready, 1)

            def late_pair(m, j):
                pair_gate(m, j, j % 2)
                pair_up(m, j, j % 2)
                pair_weigh(m, j, j % SLOTS, j // SLOTS + 1)

            setup()
            for k in range(QUARTERS):
                pre_piece(0, k)
                if k == 4:
                    setup_attention()
                elif k == 16:
                    setup_rest()
            for p in range(CH + 1):
                scan, moe = p < CH, p > 0
                m = p - 1

                def quarter(i, c):
                    pair = moe and not (isinstance(i, int) and i == 0)
                    j = (i - 1) * SLOTS + c
                    if scan:
                        inputs(p, i, c)
                        if not moe and (i > 0 or c > 0):
                            beside(i * SLOTS + c - 1)
                        unit(p, i, c, 0)
                    if pair:
                        pair_gate(m, j, c % 2)
                        pair_up(m, j, c % 2)
                    if scan:
                        unit(p, i, c, 1)
                    if pair:
                        pair_weigh(m, j, c, i)

                def piece(k):
                    if moe:
                        beside(k)

                def beside(k):
                    if moe:
                        router(m, k)
                        if m >= 1 and k == 0:
                            finish(m - 1)
                    if scan:
                        gate_piece(p, k)
                    if p + 1 < CH and (moe or k - 1 < 26):
                        pre_piece(p + 1, k - 1)

                at_quarters(dve, p, quarter, piece)
                late = list(range(PAIRS - LATE, PAIRS)) if moe else []
                for j in late[:2]:
                    late_pair(m, j)
                if not moe:
                    for k in range(26, 29):
                        pre_piece(1, k)
                if scan:
                    gating(p)
                if not moe:
                    for k in range(29, QUARTERS):
                        pre_piece(1, k)
                for j in late[2:3]:
                    late_pair(m, j)
                if scan:
                    residual(p)
                for j in late[3:]:
                    late_pair(m, j)
            finish(CH - 1)

        @block.tensor
        def _(pe):
            mm = nc.tensor.matmul

            def setup():
                for signal in pair_done + summed:
                    pe.sem_inc(signal, FREE)
                pe.wait_ge(zeros_ready, 1)
                keep_busy(bank[7], 8)
                pe.wait_ge(cond_in, 16 * (KH + 1))
                pe.wait_ge(silu_c_rep, 1)
                modulation(SA, GA).then_inc(mod_ready, 1)
                keep_busy(bank[7], 8)
                pe.wait_ge(ident_ready, 2)

            def keep_busy(ps, count):
                for _ in range(count):
                    mm(ps[:], zeros_bf[:, 0:P], zeros_bf[:], start=True, stop=True)

            def modulation(first, end):
                for j in range(first * KH, end * KH):
                    for k in range(KH):
                        last = mm(gate_ps[0][:, j:j + 1], wmod_sb(k)[:, j * P:(j + 1) * P], c_rep[:, k, 0:1],
                                  start=(k == 0), stop=(k == KH - 1))
                return last

            def modulation_rest():
                pe.wait_ge(weights_in, NLOAD)
                pe.wait_ge(dve_setup, 1)
                modulation(GA, 6)
                for k in range(KH):
                    last = mm(gate_ps[1][:, 0:H], c_rep[:, k, :], wmod_sb(k)[:, GA * H:(GA + 1) * H],
                              start=(k == 0), stop=(k == KH - 1))
                last.then_inc(mod_ready, 1)

            def piece_free(index):
                if index > 1:
                    pe.wait_ge(piece_read, index - pieces_in_flight(index))

            def in_proj_piece(index, b):
                piece_free(index)
                for kh in range(KH):
                    last = mm(piece_bank(index)[:], w_in[:, kh, b * P:(b + 1) * P], h_attn[:, kh, :],
                              start=(kh == 0), stop=(kh == KH - 1))
                last.then_inc(piece_ready, 1)

            def gate_piece(p, k):
                if k < DB:
                    in_proj_piece(p * ROUND + PIECES + k, DB + k)

            def pre_piece(c, k):
                first = c * ROUND
                if 5 <= k < 5 + KH:
                    kh = k - 5
                    index = first + kh
                    piece_free(index)
                    pe.wait_ge(xn_ready, c + 1)
                    for t in range(TT):
                        last = nc.tensor.transpose(piece_bank(index)[:, t * P:(t + 1) * P],
                                                   x_norm[:, t, kh * P:(kh + 1) * P], ident[:])
                    last.then_inc(piece_ready, 1)
                elif 8 <= k < 8 + DB:
                    if k == 8:
                        pe.wait_ge(piece_read, first + KH)
                        pe.wait_ge(conv_in, 16 * 3)
                    in_proj_piece(first + KH + k - 8, k - 8)
                elif k in (17, 23):
                    index = first + (KH + DB if k == 17 else PIECES - 1)
                    piece_free(index)
                    rows = slice(0, R) if k == 17 else slice(R, R + 2 * N)
                    dst = piece_bank(index)[:] if k == 17 else piece_bank(index)[0:2 * N, :]
                    for b in range(DB):
                        pe.wait_ge(u_ready, c * DB + b + 1)
                        last = mm(dst, w_xp[:, b, rows], u[:, b, :], start=(b == 0), stop=(b == DB - 1))
                    last.then_inc(piece_ready, 1)
                elif 19 <= k < 19 + DB:
                    b = k - 19
                    index = first + KH + DB + 1 + b
                    piece_free(index)
                    pe.wait_ge(piece_read, first + KH + DB + 1)
                    mm(piece_bank(index)[:], w_dt[:, b * P:(b + 1) * P], dt_low[:], start=True, stop=True) \
                        .then_inc(piece_ready, 1)

            def gate_up(m, j, s, arrivals):
                q = s % 2
                pe.wait_ge(gu_arrived[s], (arrivals + m * LOADS[s]) * 16)
                if isinstance(j, int) and j == 1 and m + 1 < CH:
                    pe.wait_ge(scan_done, ((m + 1) * BODIES + 1) * 2 * SLOTS + 2 * FREE)
                if isinstance(j, int) and j < 2:
                    pe.wait_ge(inter_ready, m * PAIRS + 2 * FREE)
                else:
                    pe.wait_ge(inter_ready, j + m * PAIRS - 1 + 2 * FREE)
                if is_shared(j):
                    for half, done in ((slice(0, T // 2), gate_ready), (slice(T // 2, T), up_ready)):
                        for k in range(KH):
                            last = mm(gate_ps[q][:, half], w_gu[:, s, k * 2 * P:k * 2 * P + P], h_moe[:, k, half],
                                      start=(k == 0), stop=(k == KH - 1))
                        last.then_inc(done, 1)
                    return
                for ps, o, done in ((gate_ps[q], 0, gate_ready), (up_ps[q], P, up_ready)):
                    for k in range(KH):
                        last = mm(ps[:], w_gu[:, s, k * 2 * P + o:k * 2 * P + o + P], h_moe[:, k, :],
                                  start=(k == 0), stop=(k == KH - 1))
                    last.then_inc(done, 1)

            def down(m, j, s, arrivals):
                stop = is_shared(j)
                rows = rows_of(j)
                pe.wait_ge(down_arrived[s], (arrivals + m * LOADS[s]) * 16)
                pe.wait_ge(inter_ready, j + m * PAIRS + 1 + 2 * FREE)
                for k in range(KH):
                    last = mm(out_ps[k][:], w_down[rows, s, k * P:(k + 1) * P], inter[rows, s % 2, :],
                              start=False, stop=stop, skip_group_check=True)
                    if stop:
                        last.then_inc(o_ready, 1)
                if not stop:
                    last.then_inc(pair_done[s], 1)

            def open_sums(banks):
                for ps in banks:
                    mm(ps[:], zeros_bf[:, 0:P], zeros_bf[:], start=True, stop=False, skip_group_check=True)

            def sum_states(i, c):
                hf, r = c // 2, c % 2
                pe.wait_ge(prod_done[hf], i * 2 + r + 1 + FREE)
                for e in range(2):
                    last = mm(bank[2 * r + e][:], ident[:], prod[:, r, e, :], start=False, stop=False,
                              skip_group_check=True)
                last.then_inc(summed[r], 1)

            def out_transposes(m):
                pe.wait_ge(ofm_ready, (m + 1) * KH)
                for t in range(TT):
                    for k in range(KH):
                        last = nc.tensor.transpose(out_t_ps[t // 2][:, (t % 2) * H + k * P:(t % 2) * H + (k + 1) * P],
                                                   o_fm[:, k, t * P:(t + 1) * P], ident[:])
                        if t == 0 and k == 0:
                            last.then_inc(pair_done[0], 1)
                    if t % 2:
                        last.then_inc(oT_ready, 1)

            def attn_out(p):
                pe.wait_ge(gated, p + 1)
                for t in range(TT):
                    for b in range(DB):
                        last = mm(bank[6 + t // 2][:, (t % 2) * H:(t % 2 + 1) * H],
                                  tmp_c[:, b, t * P:(t + 1) * P],
                                  w_out[:, b, :], start=(b == 0), stop=(b == DB - 1))
                    if t % 2:
                        last.then_inc(attn_ready, 1)

            def norm_transposes(p):
                pe.wait_ge(xn2_ready, p + 1)
                for k in range(KH):
                    for t in range(TT):
                        last = nc.tensor.transpose(bank[6 + k][:, t * P:(t + 1) * P],
                                                   x_norm[:, t, k * P:(k + 1) * P], ident[:])
                    last.then_inc(xn2T_ready, 1)

            def router_logits(p):
                pe.wait_ge(moe_ready, (p + 1) * KH)
                for t in range(TT):
                    for kh in range(KH):
                        last = mm(logits_ps[:, t * (E + 1):(t + 1) * (E + 1)],
                                  h_moe[:, kh, t * P:(t + 1) * P], w_rt[:, kh, :],
                                  start=(kh == 0), stop=(kh == KH - 1))
                last.then_inc(logits_ready, 1)

            def router(p, k):
                if k == 2:
                    pe.wait_ge(wtok_ready, p + 1)
                    for t in range(TT):
                        last = nc.tensor.transpose(w_ps[0:E + 2, t * P:(t + 1) * P], w_tok[:, t, :], ident[:])
                    last.then_inc(wT_ready, 1)

            def late_down(m, j):
                down(m, j, j % SLOTS, j // SLOTS + 1)

            def late_gate_up(m, j):
                gate_up(m, j, j % SLOTS, j // SLOTS + 1)

            setup()
            for k in range(QUARTERS):
                if k == 16:
                    modulation_rest()
                pre_piece(0, k)
            pe.wait_ge(setup_done, 1)
            for b in range(DB):
                mm(bank[b][:], d_diag[:, b, :], u[:, b, :], start=True, stop=False, skip_group_check=True)
            for p in range(CH + 1):
                scan, moe = p < CH, p > 0
                m = p - 1

                def quarter(i, c):
                    if moe and not (isinstance(i, int) and i == 0):
                        t = (c + 1) % SLOTS
                        gate_up(m, (i - 1) * SLOTS + c + 1, t, i + (1 if t == 0 else 0))
                        if not isinstance(i, int) or i > 1 or c > 0:
                            down(m, (i - 1) * SLOTS + c - 1, (c - 1) % SLOTS, i if c > 0 else i - 1)

                def piece(k):
                    if moe:
                        if m >= 1 and k == 0:
                            out_transposes(m - 1)
                        if k == 2:
                            if m >= 1:
                                pe.wait_ge(out_ready, m * (TT // 2))
                            gate_up(m, 0, 0, 1)
                        router(m, k)
                        if k == 1:
                            keep_busy(w_ps, 6)
                        elif k == SLOTS:
                            pe.wait_ge(w_fm_ready, p)
                            if scan:
                                pe.wait_ge(piece_read, p * ROUND + PIECES + DB)
                            open_sums(out_ps)
                            if not scan:
                                keep_busy(bank[7], 14)
                    if scan:
                        gate_piece(p, k)
                    if p + 1 < CH:
                        pre_piece(p + 1, k - 1)
                    if not moe and k > 0:
                        sum_states((k - 1) // SLOTS, (k - 1) % SLOTS)

                at_quarters(pe, p, quarter, piece)
                if not moe:
                    sum_states(BODIES - 1, SLOTS - 1)
                    keep_busy(bank[4], 14)
                last = PAIRS - 1
                if moe:
                    late_gate_up(m, last - 3)
                    late_down(m, last - 5)
                    late_gate_up(m, last - 2)
                    late_down(m, last - 4)
                if scan:
                    attn_out(p)
                if moe:
                    late_down(m, last - 3)
                    late_gate_up(m, last - 1)
                    late_down(m, last - 2)
                    late_gate_up(m, last)
                if not moe:
                    keep_busy(bank[4], 24)
                if scan:
                    norm_transposes(p)
                if moe:
                    late_down(m, last - 1)
                if scan:
                    router_logits(p)
                if moe:
                    late_down(m, last)
            out_transposes(CH - 1)


_OUT = ((1, 2048, 256), "float32")


def kernel(**inputs):
    import numpy as _np
    import concourse.bacc as _bacc
    from concourse import mybir as _mybir
    from concourse.bass_utils import run_bass_kernel_spmd as _run

    def rows(a):
        return _np.ascontiguousarray(a.reshape(a.shape[0] // 128, 128, -1).transpose(1, 0, 2))

    def cols(a):
        return _np.ascontiguousarray(a.reshape(-1, 128).T)

    a = {k: _np.asarray(x) for k, x in inputs.items()}
    gu, dp = a["L0_ffn_gu_w"], a["L0_ffn_dp_w"]
    E, I2, H = gu.shape
    inner = I2 // 2
    gate = _np.concatenate([gu[:, :inner], a["L0_ffn_sh_gate_w"][None], a["L0_ffn_sh_up_w"][None]])
    up = _np.concatenate([gu[:, inner:], _np.zeros((2, inner, H), gu.dtype)])
    down = _np.concatenate([dp, a["L0_ffn_sh_down_w"][None], _np.zeros((1, H, inner), dp.dtype)])
    pairs = (E + 2) // 2

    def lhs(w):
        return w.reshape(pairs, 128, H // 128, 128).transpose(0, 3, 2, 1)

    gate_up = _np.stack([lhs(gate), lhs(up)], axis=3).reshape(pairs, 128, -1)
    downs = down.transpose(0, 2, 1).reshape(pairs, 128, H)
    arrays = {
        "x_in": _np.ascontiguousarray(a["L0_attn_hidden_states"].reshape(-1, H)),
        "in_proj": rows(a["L0_attn_in_proj_w"].T),
        "conv_w": rows(a["L0_attn_conv_w"].reshape(-1, a["L0_attn_conv_w"].shape[2])),
        "conv_b": cols(a["L0_attn_conv_b"]),
        "x_proj": rows(a["L0_attn_x_proj_w"].T),
        "dt_proj": _np.ascontiguousarray(a["L0_attn_dt_proj_w"].T),
        "dt_b": cols(a["L0_attn_dt_proj_b"]),
        "a_log": rows(a["L0_attn_A_log"]),
        "d_skip": cols(a["L0_attn_D"]),
        "out_proj": rows(a["L0_attn_out_proj_w"].T),
        "router": rows(_np.concatenate([a["L0_ffn_gate_w"], a["L0_ffn_sh_gate1_w"]]).T),
        "pair_w": _np.ascontiguousarray(_np.concatenate([gate_up, downs], axis=2)),
        "cond": cols(a["L0_c"].reshape(-1)),
        "wmod": rows(a["L0_wmod"]),
    }
    nc = _bacc.Bacc("TRN2", target_bir_lowering=False, num_devices=1)
    args = [nc.dram_tensor(n, x.shape, _mybir.dt.from_np(x.dtype), kind="ExternalInput").ap()
            for n, x in arrays.items()]
    shape, dtype = _OUT
    out = nc.dram_tensor("out_0_dram", shape, _mybir.dt.from_np(_np.dtype(dtype)), kind="ExternalOutput").ap()
    adaln_mamba_moe(nc, *args, out.rearrange("b l h -> (b l) h"))
    r = _run(nc, [arrays], core_ids=[0])
    return r.results[0]["out_0_dram"]
```
